# Optimizing a Trainium2 kernel written in Bass

```python
import numpy as np
import jax
import jax.numpy as jnp

def _softmax(x, axis=-1):
    return jax.nn.softmax(x, axis=axis)

def _gelu(x):
    return jax.nn.gelu(x, approximate=True)

def _silu(x):
    return jax.nn.silu(x)

def _sigmoid(x):
    return jax.nn.sigmoid(x)

def _layernorm(x, axis=-1, eps=1e-05):
    m = jnp.mean(x, axis=axis, keepdims=True)
    v = jnp.var(x, axis=axis, keepdims=True)
    return (x - m) / jnp.sqrt(v + eps)

def _scatter_add(tgt, idx, src, axis=0):
    return tgt.at[idx].add(src)

def _segment_sum(src, seg, n):
    return jax.ops.segment_sum(src, seg, n)
kernel_name = 'mk_gnn_preln_d1_gnn_r8_41352e'

def setup_inputs(seed: int=0):
    np.random.seed(seed)
    _w = jnp.asarray

    def _rec_inputs():
        import jax
        import jax.numpy as jnp
        _gk = jax.random.key(seed)
        x = -0.0004287 + 1 * jax.random.normal(jax.random.fold_in(_gk, 1), (12500, 160), jnp.float32)
        src = jax.random.randint(jax.random.fold_in(_gk, 2), (200000,), 0, 12500, jnp.int32)
        dst = jnp.minimum((12500 * jax.random.uniform(jax.random.fold_in(_gk, 3), (200000,)) ** 2.0).astype(jnp.int32), 99999)
        _o = jnp.argsort(dst, stable=True)
        src = src[_o]
        dst = dst[_o]
        edge_attr_10 = jax.random.uniform(jax.random.fold_in(_gk, 12), (200000, 10), jnp.float32, 0.0, 1)
        edge_attr_4 = 0.000486536 + 0.999406 * jax.random.normal(jax.random.fold_in(_gk, 13), (200000, 4), jnp.float32)
        node_vec1 = -0.00786984 + 0.999612 * jax.random.normal(jax.random.fold_in(_gk, 14), (12500, 1), jnp.float32)
        node_vec1_n2 = -0.00786984 + 0.999612 * jax.random.normal(jax.random.fold_in(_gk, 15), (12500, 1), jnp.float32)
        node_vec1_n3 = -0.00786984 + 0.999612 * jax.random.normal(jax.random.fold_in(_gk, 16), (12500, 1), jnp.float32)
        return (x, src, dst, edge_attr_10, edge_attr_4, node_vec1, node_vec1_n2, node_vec1_n3)
    x, src, dst, edge_attr_10, edge_attr_4, node_vec1, node_vec1_n2, node_vec1_n3 = _rec_inputs()

    def _L0_gnn_setup():
        import jax, jax.numpy as jnp
        import numpy as np
        N = 3125
        E = 50000
        S = 64
        V = 32
        NB = 10
        H = 100
        WN = 192
        MID = 96
        NUM_NEIGHBORS = 16.0
        C_S = float(np.sin(np.pi / 8.0))
        C_X = float(np.cos(np.pi / 8.0))
        SQRT3 = float(np.sqrt(3.0))

        def fctp_scalar_attr(xs, xv, attr, Ws, Wv):
            s = xs * attr @ Ws
            v = jnp.einsum('nuc,uo->noc', xv * attr[:, :, None], Wv)
            return (s, v)
        key = jax.random.key(seed)
        k = jax.random.split(key, 24)

        def w(i, shape):
            return jax.random.normal(k[i], shape, jnp.float32) / np.sqrt(float(shape[0]))
        return {'node_input': jax.random.normal(k[0], (N, S + 3 * V), jnp.float32), 'node_attr': jax.random.normal(k[1], (N, 1), jnp.float32), 'node_crystal_attr': jax.random.normal(k[2], (N, 1), jnp.float32), 'sym_mask': jax.random.normal(k[3], (N, 1), jnp.float32), 'edge_attr': jax.random.normal(k[4], (E, 4), jnp.float32), 'edge_length_embedded': jax.random.uniform(k[5], (E, NB), dtype=jnp.float32), 'edge_src': jax.random.randint(k[6], (E,), 0, N), 'edge_dst': jax.random.randint(k[7], (E,), 0, N), 'Ws_sc_a': w(8, (S, S)), 'Wv_sc_a': w(9, (V, V)), 'Ws_sc_c': w(10, (S, S)), 'Wv_sc_c': w(11, (V, V)), 'Ws_l1_a': w(12, (S, S)), 'Wv_l1_a': w(13, (V, V)), 'Ws_l1_c': w(14, (S, S)), 'Wv_l1_c': w(15, (V, V)), 'W_fc1': w(16, (NB, H)), 'W_fc2': w(17, (H, WN)), 'Ws_l2_a': w(18, (MID, MID)), 'Wv_l2_a': w(19, (MID, MID)), 'Ws_l2_c': w(20, (MID, MID)), 'Wv_l2_c': w(21, (MID, MID)), 'Ws_l3': w(22, (MID, S)), 'Wv_l3': w(23, (MID, V))}
    _L0_gnn_all = _L0_gnn_setup()
    _L0_gnn_in = {k: v for k, v in _L0_gnn_all.items() if k in ('Ws_sc_a', 'Wv_sc_a', 'Ws_sc_c', 'Wv_sc_c', 'Ws_l1_a', 'Wv_l1_a', 'Ws_l1_c', 'Wv_l1_c', 'W_fc1', 'W_fc2', 'Ws_l2_a', 'Wv_l2_a', 'Ws_l2_c', 'Wv_l2_c', 'Ws_l3', 'Wv_l3')}
    del _L0_gnn_all
    return {'x': x, 'src': src, 'dst': dst, 'edge_attr_10': edge_attr_10, 'edge_attr_4': edge_attr_4, 'node_vec1': node_vec1, 'node_vec1_n2': node_vec1_n2, 'node_vec1_n3': node_vec1_n3, 'L0_gnn_Ws_sc_a': _L0_gnn_in['Ws_sc_a'], 'L0_gnn_Wv_sc_a': _L0_gnn_in['Wv_sc_a'], 'L0_gnn_Ws_sc_c': _L0_gnn_in['Ws_sc_c'], 'L0_gnn_Wv_sc_c': _L0_gnn_in['Wv_sc_c'], 'L0_gnn_Ws_l1_a': _L0_gnn_in['Ws_l1_a'], 'L0_gnn_Wv_l1_a': _L0_gnn_in['Wv_l1_a'], 'L0_gnn_Ws_l1_c': _L0_gnn_in['Ws_l1_c'], 'L0_gnn_Wv_l1_c': _L0_gnn_in['Wv_l1_c'], 'L0_gnn_W_fc1': _L0_gnn_in['W_fc1'], 'L0_gnn_W_fc2': _L0_gnn_in['W_fc2'], 'L0_gnn_Ws_l2_a': _L0_gnn_in['Ws_l2_a'], 'L0_gnn_Wv_l2_a': _L0_gnn_in['Wv_l2_a'], 'L0_gnn_Ws_l2_c': _L0_gnn_in['Ws_l2_c'], 'L0_gnn_Wv_l2_c': _L0_gnn_in['Wv_l2_c'], 'L0_gnn_Ws_l3': _L0_gnn_in['Ws_l3'], 'L0_gnn_Wv_l3': _L0_gnn_in['Wv_l3']}

def reference(x, src, dst, edge_attr_10, edge_attr_4, node_vec1, node_vec1_n2, node_vec1_n3, L0_gnn_Ws_sc_a, L0_gnn_Wv_sc_a, L0_gnn_Ws_sc_c, L0_gnn_Wv_sc_c, L0_gnn_Ws_l1_a, L0_gnn_Wv_l1_a, L0_gnn_Ws_l1_c, L0_gnn_Wv_l1_c, L0_gnn_W_fc1, L0_gnn_W_fc2, L0_gnn_Ws_l2_a, L0_gnn_Wv_l2_a, L0_gnn_Ws_l2_c, L0_gnn_Wv_l2_c, L0_gnn_Ws_l3, L0_gnn_Wv_l3):
    import jax
    import jax.numpy as jnp

    def _L0_gnn_ref(node_input, node_attr, node_crystal_attr, sym_mask, edge_attr, edge_length_embedded, edge_src, edge_dst, Ws_sc_a, Wv_sc_a, Ws_sc_c, Wv_sc_c, Ws_l1_a, Wv_l1_a, Ws_l1_c, Wv_l1_c, W_fc1, W_fc2, Ws_l2_a, Wv_l2_a, Ws_l2_c, Wv_l2_c, Ws_l3, Wv_l3):
        import jax, jax.numpy as jnp
        import numpy as np
        N = 3125
        E = 50000
        S = 64
        V = 32
        NB = 10
        H = 100
        WN = 192
        MID = 96
        NUM_NEIGHBORS = 16.0
        C_S = float(np.sin(np.pi / 8.0))
        C_X = float(np.cos(np.pi / 8.0))
        SQRT3 = float(np.sqrt(3.0))

        def fctp_scalar_attr(xs, xv, attr, Ws, Wv):
            s = xs * attr @ Ws
            v = jnp.einsum('nuc,uo->noc', xv * attr[:, :, None], Wv)
            return (s, v)
        n = node_input.shape[0]
        xs = node_input[:, :S]
        xv = node_input[:, S:].reshape(n, V, 3)
        ssa, sva = fctp_scalar_attr(xs, xv, node_attr, Ws_sc_a, Wv_sc_a)
        ssc, svc = fctp_scalar_attr(xs, xv, node_crystal_attr, Ws_sc_c, Wv_sc_c)
        s_s, s_v = (ssa + ssc, sva + svc)
        l1a_s, l1a_v = fctp_scalar_attr(xs, xv, node_attr, Ws_l1_a, Wv_l1_a)
        l1c_s, l1c_v = fctp_scalar_attr(xs, xv, node_crystal_attr, Ws_l1_c, Wv_l1_c)
        x1s, x1v = (l1a_s + l1c_s, l1a_v + l1c_v)
        weight = jax.nn.silu(edge_length_embedded @ W_fc1) @ W_fc2
        w0 = weight[:, :S]
        w1 = weight[:, S:2 * S]
        w2 = weight[:, 2 * S:2 * S + V]
        w3 = weight[:, 2 * S + V:]
        gs = x1s[edge_src]
        gv = x1v[edge_src]
        e_s = edge_attr[:, :1]
        e_v = edge_attr[:, 1:]
        mid0a = w0 * gs * e_s
        mid0b = w3 * (jnp.einsum('euc,ec->eu', gv, e_v) / SQRT3)
        mid1a = w1[:, :, None] * gs[:, :, None] * e_v[:, None, :]
        mid1b = w2[:, :, None] * gv * e_s[:, :, None]
        edge_feat = jnp.concatenate([mid0a, mid0b, mid1a.reshape(-1, 3 * S), mid1b.reshape(-1, 3 * V)], axis=-1)
        agg = jax.ops.segment_sum(edge_feat, edge_dst, num_segments=n) / np.sqrt(NUM_NEIGHBORS)
        m_s = agg[:, :MID]
        m_v = agg[:, MID:].reshape(n, MID, 3)
        l2a_s, l2a_v = fctp_scalar_attr(m_s, m_v, node_attr, Ws_l2_a, Wv_l2_a)
        l2c_s, l2c_v = fctp_scalar_attr(m_s, m_v, node_crystal_attr, Ws_l2_c, Wv_l2_c)
        m_s, m_v = (l2a_s + l2c_s, l2a_v + l2c_v)
        o_s, o_v = fctp_scalar_attr(m_s, m_v, sym_mask, Ws_l3, Wv_l3)
        out_s = C_S * s_s + C_X * o_s
        out_v = C_S * s_v + C_X * o_v
        return jnp.concatenate([out_s, out_v.reshape(n, 3 * V)], axis=-1)
    h = jnp.maximum(_layernorm(x, axis=-1), 0.0)
    x = x + _L0_gnn_ref(h, node_vec1, node_vec1_n2, node_vec1_n3, edge_attr_4, edge_attr_10, src, dst, L0_gnn_Ws_sc_a, L0_gnn_Wv_sc_a, L0_gnn_Ws_sc_c, L0_gnn_Wv_sc_c, L0_gnn_Ws_l1_a, L0_gnn_Wv_l1_a, L0_gnn_Ws_l1_c, L0_gnn_Wv_l1_c, L0_gnn_W_fc1, L0_gnn_W_fc2, L0_gnn_Ws_l2_a, L0_gnn_Wv_l2_a, L0_gnn_Ws_l2_c, L0_gnn_Wv_l2_c, L0_gnn_Ws_l3, L0_gnn_Wv_l3)
    return x

_drawn_inputs = setup_inputs


def setup_inputs(seed=0):
    import zlib

    import numpy as np

    out = dict(_drawn_inputs(seed))
    spreads = {}
    factors = {}
    for name, (base, spread) in spreads.items():
        noise = np.random.default_rng([zlib.crc32(name.encode()), seed]).standard_normal(out[name].shape)
        drawn = base * np.exp(spread * noise) if base else spread * noise
        out[name] = jnp.asarray(drawn.astype(out[name].dtype))
    for name, factor in factors.items():
        out[name] = (out[name] * factor).astype(out[name].dtype)
    return out
```

```python
import concourse.bass as bass
from concourse import mybir
from contextlib import ExitStack
import math

fp32 = mybir.dt.float32
bf16 = mybir.dt.bfloat16
i32 = mybir.dt.int32
ALU = mybir.AluOpType
ACT = mybir.ActivationFunctionType
AX = mybir.AxisListType

N, E, S, V, NBAS, H, MID = 12500, 200000, 64, 32, 10, 100, 96
D = S + 3 * V
P = 128
NB = -(-N // P)
LAST = N - P
U = -(-E // (2 * P))
EP = U * 2 * P
UG = 17
UP = U // UG
C_S = math.sin(math.pi / 8.0)
C_X = math.cos(math.pi / 8.0)
AVG = 4.0
LN_CHUNK = 7
NCH = NB // LN_CHUNK
RING = 4
LAG = 2
WS, WV = 160, 96


def gnn_kernel(nc, x, dst_u, dst_t, src_t, attr_t, len_T, nv, w, out):
    assert UP * UG == U and NCH * LN_CHUNK == NB
    x1 = nc.dram_tensor("x1_table", (N, D), fp32).ap()
    tmm = nc.dram_tensor("pair_min_max", (2, U), fp32).ap()
    rng = nc.dram_tensor("window_ranges", (NB, 4), i32).ap()

    ctx = ExitStack()
    with ctx:
        def sb(name, shape, dt=fp32):
            return ctx.enter_context(nc.sbuf_tensor(name, shape, dt))

        def sem(name):
            return ctx.enter_context(nc.semaphore(name))

        bank = [ctx.enter_context(nc.psum_tensor(f"bank{i}", [P, 512], fp32)) for i in range(8)]

        base = sb("base", [P, NB, D])
        xc = sb("xc", [P, NB, D])
        stat = sb("stat", [P, 4, LN_CHUNK])
        rstd = sb("rstd", [P, NB])
        nvs = sb("nvs", [P, 3, NB])
        arcr = sb("arcr", [P, 2, NB])
        uauc = sb("uauc", [P, 2, NB])
        xs = sb("xs", [P, 2, D])
        hT = sb("hT", [P, 2, 2 * P])
        part = sb("part", [P, 2, 2 * D])
        scs = sb("scs", [P, 2, D])
        wn1 = sb("wn1", [P, 512])
        wn2 = sb("wn2", [V, 128])
        wl2 = sb("wl2", [MID, 4, MID])
        wl3s = sb("wl3s", [MID, S])
        wl3v = sb("wl3v", [MID, V])
        fold = sb("fold", [MID, 2 * S + 2 * V])
        wfc1 = sb("wfc1", [NBAS, H])
        wfc2 = sb("wfc2", [H, 192])
        src = sb("src", [P, 2 * U], i32)
        dstf = sb("dstf", [P, 2 * U])
        attr = sb("attr", [P, 2 * U, 4])
        idx = sb("idx", [P, RING, 2], i32)
        lenr = sb("lenr", [NBAS, RING, 2 * P])
        G = sb("G", [P, RING, 2, D])
        sq = G[:].rearrange("p r j f -> p (r j) f")[:, 0:LN_CHUNK, :]
        hid = sb("hid", [H, 2 * P])
        sel = sb("sel", [P, 2, 4, P])
        prod = sb("prod", [P, 2, 2 * WS + 2 * WV])
        agg = sb("agg", [P, 4, MID])
        aggT = sb("aggT", [MID, 4 * P])
        outs = sb("outs", [P, D])
        zero = sb("zero", [1, 512], bf16)
        ident = sb("ident", [P, P])
        iota_i = sb("iota_i", [P, P], i32)
        iota_f = sb("iota_f", [P, P])
        iota_w = sb("iota_w", [P, P])
        part_f = sb("part_f", [P, 1])
        xflat = xc[:].rearrange("p w f -> p (w f)")
        o = UG * 2 * P
        dstu = xflat[0:UP, 0:o].bitcast(i32).rearrange("p (g e) -> p g e", g=UG)
        mmb = xflat[0:NB, o:o + 2 * U].rearrange("p (k u) -> p k u", k=2)
        pos_i = xflat[0:NB, o + 2 * U:o + 3 * U].bitcast(i32)
        pos = xflat[0:NB, o + 3 * U:o + 4 * U]
        dst_i = xflat[:, o + 4 * U:o + 6 * U].bitcast(i32)
        mm = sb("mm", [UP, 2, UG])
        wst = sb("wst", [P, NB])
        wst_c = sb("wst_c", [NB, 2])
        hl = sb("hl", [NB, 4])
        tri = sb("tri", [NB, NB])
        rngc = sb("rngc", [NB, 4], i32)
        row = sb("row", [1, NB * 4], i32)

        in_loaded = sem("in_loaded")
        x_loaded = sem("x_loaded")
        dstu_loaded = sem("dstu_loaded")
        zeroed = sem("zeroed")
        iotas = sem("iotas")
        consts = sem("consts")
        mm_done = sem("mm_done")
        mm_stored = sem("mm_stored")
        mm_loaded = sem("mm_loaded")
        cnt_done = sem("cnt_done")
        cum_done = sem("cum_done")
        rng_done = sem("rng_done")
        rng_stored = sem("rng_stored")
        row_loaded = sem("row_loaded")
        fold_mm = sem("fold_mm")
        fold_done = sem("fold_done")
        xc_ready = sem("xc_ready")
        sq_done = sem("sq_done")
        var_done = sem("var_done")
        std_done = sem("std_done")
        ln_done = sem("ln_done")
        xs_ready = sem("xs_ready")
        xs_free = sem("xs_free")
        h_t = sem("h_t")
        h_evac = sem("h_evac")
        n_mm = sem("n_mm")
        n_part = sem("n_part")
        n_done = [sem(f"n_done{q}") for q in range(2)]
        x1_ready = sem("x1_ready")
        x1_stored = sem("x1_stored")
        idx_loaded = [sem(f"idx_loaded{k}") for k in range(RING)]
        idx_free = sem("idx_free")
        len_loaded = [sem(f"len_loaded{k}") for k in range(RING)]
        len_ready = sem("len_ready")
        len_free = sem("len_free")
        gathered = [sem(f"gathered{k}") for k in range(RING)]
        g_ready = sem("g_ready")
        g_free = sem("g_free")
        pre_ready = sem("pre_ready")
        hid_ready = sem("hid_ready")
        w_ready = [sem(f"w_ready{j}") for j in range(2)]
        b_ready = [sem(f"b_ready{j}") for j in range(2)]
        dup_ready = [sem(f"dup_ready{j}") for j in range(2)]
        prod_ready = [sem(f"prod_ready{j}") for j in range(2)]
        sel_free = [sem(f"sel_free{j}") for j in range(2)]
        agg_done = sem("agg_done")
        agg_copied = sem("agg_copied")
        aggT_mm = sem("aggT_mm")
        aggT_ready = sem("aggT_ready")
        o_mm = sem("o_mm")
        out_ready = sem("out_ready")
        out_stored = sem("out_stored")

        def take(eng, s, n=1):
            eng.wait_ge(s, n).then_inc(s, -n)

        PAIRS = NB // 2
        loads = [
            (nvs[:], nv),
            (wfc1[:], w["W_fc1"]), (wfc2[:], w["W_fc2"]),
            (wl3s[:], w["Ws_l3"]), (wl3v[:], w["Wv_l3"]),
            (wl2[:, 0, :], w["Ws_l2_aT"]), (wl2[:, 1, :], w["Ws_l2_cT"]),
            (wl2[:, 2, :], w["Wv_l2_aT"]), (wl2[:, 3, :], w["Wv_l2_cT"]),
            (src[:], src_t), (dst_i, dst_t), (attr[:], attr_t),
        ]
        for half, kind in enumerate("ac"):
            o = 256 * half
            loads += [(wn1[0:64, o:o + 64], w[f"Ws_l1_{kind}"]), (wn1[0:64, o + 128:o + 192], w[f"Ws_sc_{kind}"]),
                      (wn2[:, 64 * half:64 * half + 32], w[f"Wv_l1_{kind}"]),
                      (wn2[:, 64 * half + 32:64 * half + 64], w[f"Wv_sc_{kind}"])]
            for c in range(2):
                r = slice(64 + 32 * c, 96 + 32 * c)
                loads += [(wn1[r, o + 64 + 32 * c:o + 96 + 32 * c], w[f"Wv_l1_{kind}"]),
                          (wn1[r, o + 192 + 32 * c:o + 224 + 32 * c], w[f"Wv_sc_{kind}"])]
        N_LOADS = 16 * len(loads)

        def edge_range(eng, b):
            first = eng.value_load(row[0:1, bass.ds(b * 4, 1)], min_val=0, max_val=U - 1)
            count = eng.value_load(row[0:1, bass.ds(b * 4 + 1, 1)], min_val=1, max_val=U)
            before = eng.value_load(row[0:1, bass.ds(b * 4 + 2, 1)], min_val=0, max_val=NB * U)
            return first, count, before

        def all_pairs(eng):
            _, count, before = edge_range(eng, NB - 1)
            return count + before

        block = ctx.enter_context(nc.Block())

        @block.sync
        def _(sp):
            sp.dma_start(dstu, dst_u).then_inc(dstu_loaded, 16)
            whole = x[0:(NB - 1) * P, :].rearrange("(w p) f -> p w f", p=P)
            for ch in range(NCH):
                a, z = ch * LN_CHUNK, min((ch + 1) * LN_CHUNK, NB - 1)
                sp.dma_start(base[:, a:z, :], whole[:, a:z, :]).then_inc(x_loaded, 16)
            sp.dma_start(base[:, NB - 1, :], x[LAST:N, :]).then_inc(x_loaded, 16)
            sp.wait_ge(zeroed, 1)
            for to, fr in loads:
                sp.dma_start(to, fr).then_inc(in_loaded, 16)
            sp.wait_ge(mm_done, 1)
            for k in range(2):
                sp.dma_start(tmm[k].rearrange("(p g) -> p g", g=UG), mm[:, k, :]).then_inc(mm_stored, 16)
            sp.wait_ge(mm_stored, 32)
            sp.dma_start(mmb, tmm.unsqueeze(0).to_broadcast([NB, 2, U])).then_inc(mm_loaded, 16)
            sp.wait_ge(rng_done, 1)
            sp.dma_start(rng, rngc[:]).then_inc(rng_stored, 16)
            sp.wait_ge(rng_stored, 16)
            sp.dma_start(row[:], rng.rearrange("b k -> (b k)").unsqueeze(0)).then_inc(row_loaded, 16)
            for ch in range(NCH):
                a, z = ch * LN_CHUNK, min((ch + 1) * LN_CHUNK, NB - 1)
                sp.wait_ge(x1_ready, (z - a) + a)
                sp.dma_start(x1[0:(NB - 1) * P, :].rearrange("(w p) f -> p w f", p=P)[:, a:z, :],
                             xc[:, a:z, :]).then_inc(x1_stored, 16)
            sp.wait_ge(x1_ready, NB)
            sp.wait_ge(x1_stored, 16 * NCH)
            sp.dma_start(x1[LAST:N, :], xc[:, NB - 1, :]).then_inc(x1_stored, 16)

            sp.wait_ge(row_loaded, 16)
            sp.wait_ge(in_loaded, N_LOADS)

            def issue(k, u):
                sp.dma_start(idx[:, k, :], src[:, bass.ds(u * 2, 2)]).then_inc(idx_loaded[k], 16)
                sp.dma_start(lenr[:, k, :], len_T[:, bass.ds(u * 2 * P, 2 * P)]).then_inc(len_loaded[k], 16)
                take(sp, len_loaded[(k - 1) % RING], 16)
                sp.sem_inc(len_ready, 1)

            def load_pair(step, u):
                take(sp, idx_free)
                take(sp, len_free)
                slot = sp.snap(step & (RING - 1))
                with sp.If(slot < 2):
                    with sp.If(slot < 1):
                        issue(0, u)
                    with sp.Else():
                        issue(1, u)
                    sp.nop()
                with sp.Else():
                    with sp.If(slot < 3):
                        issue(2, u)
                    with sp.Else():
                        issue(3, u)
                    sp.nop()

            sp.sem_inc(len_loaded[RING - 1], 16)
            sp.sem_inc(idx_free, RING)
            sp.sem_inc(len_free, RING)
            with sp.Fori(0, NB) as b:
                first, count, before = edge_range(sp, b)
                with sp.Fori(0, count) as i:
                    load_pair(before + i, (first + i).with_bounds(min_val=0, max_val=U - 1))
            total = all_pairs(sp)
            with sp.Fori(0, sp.snap((((total + RING) >> 2) << 2) - total)) as i:
                load_pair(total + i, i.with_bounds(min_val=0, max_val=RING))
            take(sp, len_loaded[RING - 1], 16)
            sp.sem_inc(len_ready, 1)

        @block.gpsimd
        def _(pool):
            nc.gpsimd.memset(wn1[:], 0.0).then_inc(zeroed, 1)
            nc.gpsimd.iota(iota_i[:], [[1, P]], base=0, channel_multiplier=0).then_inc(iotas, 1)
            nc.gpsimd.iota(pos_i, [[1, U]], base=0, channel_multiplier=0).then_inc(iotas, 1)
            nc.gpsimd.memset(ident[:], 0.0).then_inc(iotas, 1)
            pool.wait_ge(iotas, 3)
            nc.gpsimd.affine_select(out=ident[:], in_=ident[:], compare_op=ALU.not_equal, fill=1.0, base=0,
                                    pattern=[[-1, P]], channel_multiplier=1).then_inc(consts, 1)
            nc.gpsimd.memset(tri[:], 1.0).then_inc(iotas, 1)
            pool.wait_ge(iotas, 4)
            nc.gpsimd.affine_select(out=tri[:], in_=tri[:], compare_op=ALU.is_gt, fill=0.0, base=0,
                                    pattern=[[1, NB]], channel_multiplier=-1).then_inc(consts, 1)
            nc.gpsimd.memset(zero[:], 0.0).then_inc(consts, 1)

            pool.wait_ge(ln_done, 1)
            pool.sem_inc(xs_free, 2)
            with pool.Fori(0, PAIRS) as p:
                for q in range(2):
                    take(pool, xs_free)
                    nc.gpsimd.tensor_copy(xs[:, q, :],
                                          xc[:, bass.ds(p * 2 + q, 1), :].rearrange("p o f -> p (o f)")
                                          ).then_inc(xs_ready, 1)

            pool.wait_ge(row_loaded, 16)
            rounds = pool.snap((all_pairs(pool) + RING) >> 2)
            pool.wait_ge(x1_stored, 16 * (NCH + 1))

            def round_(g):
                for k in range(RING):
                    take(pool, idx_loaded[k], 16)
                    take(pool, g_free)
                    for j in range(2):
                        pool.indirect_dma_start(
                            out=G[:, k, j, :], out_offset=None, in_=x1,
                            in_offset=bass.IndirectOffsetOnAxis(ap=idx[:, k, j:j + 1], axis=0),
                        ).then_inc(gathered[k], 16)
                    if k >= LAG:
                        pool.wait_ge(gathered[k - LAG], g * 32 + 32).then_inc(g_ready, 1)
                        pool.sem_inc(idx_free, 1)
                    elif not isinstance(g, int):
                        pool.wait_ge(gathered[k - LAG + RING], g * 32).then_inc(g_ready, 1)
                        pool.sem_inc(idx_free, 1)

            round_(0)
            with pool.Fori(1, rounds) as g:
                round_(g)
            for k in range(RING - LAG, RING):
                pool.wait_ge(gathered[k], rounds * 32).then_inc(g_ready, 1)
                pool.sem_inc(idx_free, 1)

        @block.scalar
        def _(act):
            for ch in range(NCH):
                a = ch * LN_CHUNK
                act.wait_ge(xc_ready, ch + 1)
                if ch:
                    act.wait_ge(var_done, ch)
                nc.scalar.activation(sq, xc[:, a:a + LN_CHUNK, :], ACT.Square).then_inc(sq_done, 1)
                act.wait_ge(var_done, ch + 1)
                nc.scalar.activation(stat[:, 3, :], stat[:, 2, :], ACT.Sqrt).then_inc(std_done, 1)

            def node_pair(w0):
                for q in range(2):
                    take(act, h_t)
                    act.sem_inc(xs_free, 1)
                    nc.scalar.activation(hT[:, q, 0:P], bank[q][:, 0:P], ACT.Relu)
                    nc.scalar.activation(hT[0:V, q, P:2 * P], bank[q][0:V, P:2 * P], ACT.Relu).then_inc(h_evac, 1)
                for q in range(2):
                    take(act, n_mm)
                    ar = arcr[:, 0, bass.ds(w0 + q, 1)]
                    to = part[:, q, :].rearrange("p (k f) -> p k f", k=2)
                    nc.scalar.activation(to[:, :, 0:128], bank[2 + q][:, 0:256].rearrange("p (k f) -> p k f", k=2),
                                         ACT.Copy, scale=ar)
                    nc.scalar.activation(to[:, :, 128:160], bank[4 + q][:, 0:64].rearrange("p (k f) -> p k f", k=2),
                                         ACT.Copy, scale=ar).then_inc(n_part, 1)

            act.wait_ge(ln_done, 1)
            with act.Fori(0, PAIRS) as p:
                node_pair(p * 2)

            act.wait_ge(fold_mm, 1)
            nc.scalar.activation(fold[0:64, 0:128], bank[6][0:64, 0:128], ACT.Copy)
            nc.scalar.activation(fold[64:96, 0:128], bank[6][64:96, 0:128], ACT.Copy, scale=1.0 / math.sqrt(3.0))
            nc.scalar.activation(fold[:, 128:192], bank[6][0:96, 128:192], ACT.Copy).then_inc(fold_done, 1)

            act.wait_ge(row_loaded, 16)

            def silu_next():
                take(act, pre_ready)
                act.sem_inc(len_free, 1)
                nc.scalar.activation(hid[:], bank[0][0:H, 0:2 * P], ACT.Silu).then_inc(hid_ready, 1)

            silu_next()
            with act.Fori(0, NB) as b:
                first, count, before = edge_range(act, b)
                with act.Fori(0, count) as i:
                    for j in range(2):
                        take(act, b_ready[j])
                        blocks = prod[:, j, WS:WS + 3 * WV].rearrange("p (c f) -> p c f", c=3)
                        nc.scalar.copy(blocks[:, 1:3, 0:S],
                                       blocks[:, 0:1, 0:S].to_broadcast([P, 2, S])).then_inc(dup_ready[j], 1)
                    silu_next()
                take(act, agg_done)
                nc.scalar.copy(agg[:, 0, 0:S], bank[3][:, 0:S])
                nc.scalar.copy(agg[:, 1:4, S:MID], bank[3][:, S:WS].rearrange("p (c f) -> p c f", c=3))
                sums = bank[3][:, WS:WS + 3 * WV].rearrange("p (c f) -> p c f", c=3)
                nc.scalar.copy(agg[:, 1:4, 0:S], sums[:, :, 0:S]).then_inc(agg_copied, 1)
                take(act, aggT_mm)
                nc.scalar.copy(aggT[:], bank[4][0:MID, :]).then_inc(aggT_ready, 1)
                take(act, out_ready)
                start = act.value_load(row[0:1, bass.ds(b * 4 + 3, 1)], min_val=0, max_val=LAST)
                act.dma_start(out[bass.ds(start, P), :], outs[:]).then_inc(out_stored, 16)

        @block.vector
        def _(dve):
            dve.wait_ge(iotas, 2)
            nc.vector.tensor_copy(iota_f[:], iota_i[:])
            nc.vector.tensor_copy(pos, pos_i)
            dve.wait_ge(dstu_loaded, 16)
            nc.vector.tensor_reduce(mm[:, 0, :], dstu, AX.X, ALU.min)
            nc.vector.tensor_reduce(mm[:, 1, :], dstu, AX.X, ALU.max).then_inc(mm_done, 1)
            dve.drain()
            nc.vector.tensor_scalar(wst[:], iota_f[:, 0:NB], float(P), float(LAST), ALU.mult, ALU.min)
            dve.wait_ge(consts, 1)
            nc.vector.tensor_tensor(iota_w[:], iota_f[:], ident[:], ALU.mult)
            dve.drain()
            nc.vector.reduce_sum(part_f[:], iota_w[:], axis=AX.X)
            dve.drain()
            nc.vector.tensor_scalar(wst_c[:, 0:1], part_f[0:NB, :], float(P), float(LAST), ALU.mult, ALU.min)
            dve.drain()
            nc.vector.tensor_scalar(wst_c[:, 1:2], wst_c[:, 0:1], float(P), None, ALU.add)
            dve.wait_ge(mm_loaded, 16)
            dve.drain()
            lo, hi = mmb[:, 0, :], mmb[:, 1, :]
            nc.vector.tensor_scalar(lo, lo, wst_c[:, 1:2], None, ALU.is_lt)
            dve.drain()
            nc.vector.scalar_tensor_tensor(out=lo, in0=hi, scalar=wst_c[:, 0:1], in1=lo, op0=ALU.is_ge, op1=ALU.mult)
            dve.drain()
            nc.vector.scalar_tensor_tensor(out=hi, in0=pos, scalar=1.0, in1=lo, op0=ALU.add, op1=ALU.mult)
            dve.drain()
            nc.vector.reduce_max(hl[:, 0:1], hi, axis=AX.X)
            dve.drain()
            nc.vector.tensor_scalar(pos, pos, -1.0, float(U), ALU.mult, ALU.add)
            dve.drain()
            nc.vector.tensor_tensor(hi, pos, lo, ALU.mult)
            dve.drain()
            nc.vector.reduce_max(hl[:, 1:2], hi, axis=AX.X)
            dve.drain()
            nc.vector.tensor_scalar(hl[:, 0:1], hl[:, 0:1], 1.0, None, ALU.max)
            nc.vector.tensor_scalar(hl[:, 1:2], hl[:, 1:2], -1.0, float(U), ALU.mult, ALU.add)
            dve.drain()
            nc.vector.tensor_scalar(hl[:, 2:3], hl[:, 0:1], 1.0, None, ALU.subtract)
            dve.drain()
            nc.vector.tensor_tensor(hl[:, 1:2], hl[:, 1:2], hl[:, 2:3], ALU.min)
            dve.drain()
            nc.vector.tensor_tensor(hl[:, 2:3], hl[:, 0:1], hl[:, 1:2], ALU.subtract).then_inc(cnt_done, 1)
            dve.wait_ge(cum_done, 1)
            nc.vector.tensor_copy(rngc[:, 0:1], hl[:, 1:2])
            dve.drain()
            nc.vector.tensor_copy(rngc[:, 1:2], hl[:, 2:3])
            nc.vector.tensor_copy(rngc[:, 3:4], wst_c[:, 0:1])
            nc.vector.tensor_copy(rngc[:, 2:3], bank[7][0:NB, 0:1]).then_inc(rng_done, 1)

            dve.wait_ge(in_loaded, N_LOADS)
            nc.vector.tensor_copy(dstf[:], dst_i)
            dve.drain()

            for ch in range(NCH):
                a = ch * LN_CHUNK
                z = a + LN_CHUNK
                dve.wait_ge(x_loaded, 16 * (NCH + 1))
                nc.vector.reduce_sum(stat[:, 0, :], base[:, a:z, :], axis=AX.X)
                dve.drain()
                nc.vector.tensor_scalar(stat[:, 1, :], stat[:, 0, :], 1.0 / D, None, ALU.mult)
                dve.drain()
                mean = stat[:, 1, :]
                nc.vector.tensor_tensor(xc[:, a:z, 0:S], base[:, a:z, 0:S],
                                        mean.unsqueeze(2).to_broadcast([P, LN_CHUNK, S]), ALU.subtract)
                nc.vector.tensor_tensor(xc[:, a:z, S:D].rearrange("p w (c u) -> p w c u", c=3),
                                        base[:, a:z, S:D].rearrange("p w (u c) -> p w c u", c=3),
                                        mean.unsqueeze(2).unsqueeze(3).to_broadcast([P, LN_CHUNK, 3, V]),
                                        ALU.subtract).then_inc(xc_ready, 1)
                dve.wait_ge(sq_done, ch + 1)
                nc.vector.reduce_sum(stat[:, 0, :], sq, axis=AX.X)
                dve.drain()
                nc.vector.tensor_scalar(stat[:, 2, :], stat[:, 0, :], 1.0 / D, 1e-5, ALU.mult,
                                        ALU.add).then_inc(var_done, 1)
                dve.wait_ge(std_done, ch + 1)
                nc.vector.reciprocal(rstd[:, a:z], stat[:, 3, :])
                dve.drain()
            for k in range(2):
                nc.vector.tensor_tensor(arcr[:, k, :], nvs[:, k, :], rstd[:], ALU.mult)
                nc.vector.scalar_tensor_tensor(out=uauc[:, k, :], in0=nvs[:, k, :], scalar=C_X / AVG,
                                               in1=nvs[:, 2, :], op0=ALU.mult, op1=ALU.mult)
            dve.drain().then_inc(ln_done, 1)

            def node_pair(w0):
                for q in range(2):
                    take(dve, n_part)
                    cr = arcr[:, 1, bass.ds(w0 + q, 1)]
                    xw = xc[:, bass.ds(w0 + q, 1), :].rearrange("p o f -> p (o f)")
                    bw = base[:, bass.ds(w0 + q, 1), :].rearrange("p o f -> p (o f)")

                    def stt(to, in0, in1):
                        return nc.vector.scalar_tensor_tensor(out=to, in0=in0, scalar=cr, in1=in1,
                                                              op0=ALU.mult, op1=ALU.add)
                    stt(scs[:, q, 0:128], bank[2 + q][:, 384:512], part[:, q, D:D + 128])
                    stt(scs[:, q, 128:160], bank[4 + q][:, 96:128], part[:, q, D + 128:D + 160])
                    stt(xw[:, 128:160], bank[4 + q][:, 64:96], part[:, q, 128:160])
                    stt(xw[:, 0:128], bank[2 + q][:, 256:384], part[:, q, 0:128]).then_inc(x1_ready, 1)
                    dve.drain()
                    nc.vector.scalar_tensor_tensor(out=bw[:, 0:S], in0=scs[:, q, 0:S], scalar=C_S, in1=bw[:, 0:S],
                                                   op0=ALU.mult, op1=ALU.add)
                    bv = bw[:, S:D].rearrange("p (u c) -> p c u", c=3)
                    nc.vector.scalar_tensor_tensor(out=bv, in0=scs[:, q, S:D].rearrange("p (c u) -> p c u", c=3),
                                                   scalar=C_S, in1=bv, op0=ALU.mult,
                                                   op1=ALU.add).then_inc(n_done[q], 1)

            with dve.Fori(0, PAIRS) as p:
                node_pair(p * 2)

            dve.wait_ge(row_loaded, 16)
            for j in range(2):
                dve.sem_inc(sel_free[j], 1)
            dve.sem_inc(g_free, RING)
            dve.sem_inc(out_stored, 16)
            dve.drain()
            with dve.Fori(0, NB) as b:
                first, count, before = edge_range(dve, b)
                nc.vector.tensor_scalar(iota_w[:], iota_f[:], wst[:, bass.ds(b, 1)], None, ALU.add)
                dve.drain()
                with dve.Fori(0, count) as i:
                    u2 = (first + i).with_bounds(min_val=0, max_val=U - 1) * 2
                    slot = dve.snap((before + i) & (RING - 1))
                    for j in range(2):
                        take(dve, sel_free[j])
                        for c in range(4):
                            nc.vector.tensor_scalar(sel[:, j, c, :], iota_w[:], dstf[:, bass.ds(u2 + j, 1)],
                                                    attr[:, bass.ds(u2 + j, 1), c], ALU.is_equal, ALU.mult)
                        if j == 0:
                            take(dve, g_ready)
                        take(dve, w_ready[j])
                        g = G[:, bass.ds(slot, 1), j, :].rearrange("p o f -> p (o f)")
                        wt = bank[1 + j]
                        pa = prod[:, j, 0:2 * WS].rearrange("p (k f) -> p k f", k=2)
                        nc.vector.tensor_tensor(pa[:, :, 0:S], wt[:, 0:2 * S].rearrange("p (k f) -> p k f", k=2),
                                                g[:, 0:S].unsqueeze(1).to_broadcast([P, 2, S]),
                                                ALU.mult).then_inc(b_ready[j], 1)
                        gv = g[:, S:D].rearrange("p (c u) -> p c u", c=3)
                        nc.vector.tensor_tensor(prod[:, j, S:WS].rearrange("p (c u) -> p c u", c=3), gv,
                                                wt[:, 128:160].unsqueeze(1).to_broadcast([P, 3, V]), ALU.mult)
                        pd = prod[:, j, WS:WS + 3 * WV].rearrange("p (c f) -> p c f", c=3)[:, :, S:MID]
                        nc.vector.tensor_tensor(pd, gv, wt[:, 160:192].unsqueeze(1).to_broadcast([P, 3, V]),
                                                ALU.mult).then_inc(prod_ready[j], 1)
                dve.wait_ge(sel_free[1], 1)
                ds_ = bank[3][:, WS:WS + 3 * WV].rearrange("p (c f) -> p c f", c=3)[:, :, S:MID]
                nc.vector.tensor_reduce(agg[:, 0, S:MID], ds_.rearrange("p c u -> p u c"), AX.X,
                                        ALU.add).then_inc(agg_done, 1)
                take(dve, out_stored, 16)
                take(dve, o_mm)
                bw = base[:, bass.ds(b, 1), :].rearrange("p o f -> p (o f)")
                ua, uc = uauc[:, 0, bass.ds(b, 1)], uauc[:, 1, bass.ds(b, 1)]
                ov = outs[:, S:D].rearrange("p (u c) -> p c u", c=3)
                pv = bank[5][:, 128:320].rearrange("p (c k u) -> p c k u", c=3, k=2)

                def stt(to, in0, scalar, in1):
                    return nc.vector.scalar_tensor_tensor(out=to, in0=in0, scalar=scalar, in1=in1, op0=ALU.mult,
                                                          op1=ALU.add)
                stt(outs[:, 0:S], bank[5][:, 0:64], ua, bw[:, 0:S])
                stt(ov, pv[:, :, 0, :], ua, bw[:, S:D].rearrange("p (u c) -> p c u", c=3))
                dve.drain()
                stt(outs[:, 0:S], bank[5][:, 64:128], uc, outs[:, 0:S])
                stt(ov, pv[:, :, 1, :], uc, ov).then_inc(out_ready, 1)
            dve.wait_ge(out_stored, 16)

        @block.tensor
        def _(pe):
            pe.wait_ge(cnt_done, 1)
            pe.wait_ge(consts, 3)
            nc.tensor.matmul(bank[7][0:NB, 0:1], tri[:], hl[:, 2:3], start=True, stop=True).then_inc(cum_done, 1)
            pe.wait_ge(in_loaded, N_LOADS)
            for k in range(2):
                nc.tensor.matmul(bank[6][0:MID, S * k:S * (k + 1)], wl2[:, k, :], wl3s[:], start=True, stop=True)
            for k in range(2):
                last = nc.tensor.matmul(bank[6][0:MID, 128 + V * k:128 + V * (k + 1)], wl2[:, 2 + k, :], wl3v[:],
                                        start=True, stop=True)
            last.then_inc(fold_mm, 1)

            def node_pair(w0):
                for q in range(2):
                    take(pe, n_done[q])
                    take(pe, xs_ready)
                    nc.tensor.transpose(bank[q][:, 0:P], xs[:, q, 0:P], ident[:])
                    nc.tensor.transpose(bank[q][0:V, P:2 * P], xs[:, q, P:D], ident[:]).then_inc(h_t, 1)
                for q in range(2):
                    take(pe, h_evac)
                    nc.tensor.matmul(bank[2 + q][:], hT[:, q, 0:P], wn1[:], start=True, stop=True)
                    nc.tensor.matmul(bank[4 + q][:, 0:128], hT[0:V, q, P:2 * P], wn2[:], start=True,
                                     stop=True).then_inc(n_mm, 1)

            pe.wait_ge(ln_done, 1)
            for q in range(2):
                pe.sem_inc(n_done[q], 1)
            with pe.Fori(0, PAIRS) as p:
                node_pair(p * 2)
            for q in range(2):
                take(pe, n_done[q])

            def first_map(step):
                take(pe, len_ready)
                slot = pe.snap(step & (RING - 1))
                nc.tensor.matmul(bank[0][0:H, 0:2 * P], wfc1[:],
                                 lenr[:, bass.ds(slot, 1), :].rearrange("p o e -> p (o e)"),
                                 start=True, stop=True).then_inc(pre_ready, 1)

            pe.wait_ge(fold_done, 1)
            take(pe, len_ready)
            first_map(0)
            with pe.Fori(0, NB) as b:
                first, count, before = edge_range(pe, b)
                nc.tensor.matmul(bank[3][:, 0:WS + 3 * WV], zero[:, 0:P], zero[:, 0:WS + 3 * WV], start=True,
                                 stop=False, skip_group_check=True)
                with pe.Fori(0, count) as i:
                    take(pe, hid_ready)
                    first_map(before + i + 1)
                    for j in range(2):
                        nc.tensor.matmul(bank[1 + j][:, 0:192], hid[:, P * j:P * (j + 1)], wfc2[:], start=True,
                                         stop=True).then_inc(w_ready[j], 1)
                    for j in range(2):
                        take(pe, prod_ready[j])
                        if j == 1:
                            pe.sem_inc(g_free, 1)
                        nc.tensor.matmul(bank[3][:, 0:WS], sel[:, j, 0, :], prod[:, j, 0:WS], start=False,
                                         stop=False, skip_group_check=True)
                        nc.tensor.matmul(bank[3][:, WS:WS + WV], sel[:, j, 1, :], prod[:, j, WS:WS + WV],
                                         start=False, stop=False, skip_group_check=True)
                        take(pe, dup_ready[j])
                        for c in range(1, 3):
                            o = WS + WV * c
                            last = nc.tensor.matmul(bank[3][:, o:o + WV], sel[:, j, 1 + c, :], prod[:, j, o:o + WV],
                                                    start=False, stop=(c == 2), skip_group_check=True)
                        last.then_inc(sel_free[j], 1)
                take(pe, agg_copied)
                for k in range(4):
                    last = nc.tensor.transpose(bank[4][0:MID, P * k:P * (k + 1)], agg[:, k, :], ident[:])
                last.then_inc(aggT_mm, 1)
                take(pe, aggT_ready)
                nc.tensor.matmul(bank[5][:, 0:128], aggT[:, 0:P], fold[:, 0:128], start=True, stop=True,
                                 skip_group_check=True)
                for c in range(3):
                    last = nc.tensor.matmul(bank[5][:, 128 + 64 * c:192 + 64 * c], aggT[:, P * (c + 1):P * (c + 2)],
                                            fold[:, 128:192], start=True, stop=True, skip_group_check=True)
                last.then_inc(o_mm, 1)


def kernel(**inputs):
    import numpy as np
    import concourse.bacc as bacc
    from concourse.bass_utils import run_bass_kernel_spmd as run

    a = {k: np.asarray(v) for k, v in inputs.items()}

    def edges(v):
        return np.pad(v, [(0, EP - E)] + [(0, 0)] * (v.ndim - 1), mode="edge")

    def lanes(v):
        v = v.reshape(2 * U, P, *v.shape[1:])
        return np.swapaxes(v, 0, 1)

    def windows(v):
        return np.concatenate([v[:(NB - 1) * P, 0].reshape(NB - 1, P).T, v[LAST:]], axis=1)

    arrays = {
        "x": a["x"],
        "dst_u": edges(a["dst"]).reshape(UP, UG, 2 * P),
        "dst_t": lanes(edges(a["dst"])),
        "src_t": lanes(edges(a["src"])),
        "attr_t": lanes(np.pad(a["edge_attr_4"], [(0, EP - E), (0, 0)])),
        "len_T": edges(a["edge_attr_10"]).T,
        "nv": np.stack([windows(a[k]) for k in ("node_vec1", "node_vec1_n2", "node_vec1_n3")], axis=1),
    }
    weights = {}
    for k, v in a.items():
        if k.startswith("L0_gnn_"):
            k = k[len("L0_gnn_"):]
            if "_l2_" in k:
                k, v = k + "T", v.T
            weights[k] = v
    nc = bacc.Bacc("TRN2", target_bir_lowering=False, num_devices=1)
    feed = {}

    def dram(name, v):
        v = np.ascontiguousarray(v)
        feed["in_" + name] = v
        return nc.dram_tensor("in_" + name, v.shape, mybir.dt.from_np(v.dtype), kind="ExternalInput").ap()

    args = {k: dram(k, v) for k, v in arrays.items()}
    w = {k: dram(k, v) for k, v in weights.items()}
    out = nc.dram_tensor("out", (N, D), fp32, kind="ExternalOutput").ap()
    gnn_kernel(nc, **args, w=w, out=out)
    return run(nc, [feed], core_ids=[0]).results[0]["out"]
```

```python
import concourse.bass as bass
from concourse import mybir
from contextlib import ExitStack
import math

fp32 = mybir.dt.float32
bf16 = mybir.dt.bfloat16
i32 = mybir.dt.int32
ALU = mybir.AluOpType
ACT = mybir.ActivationFunctionType
AX = mybir.AxisListType

N, E, S, V, NBAS, H, MID = 12500, 200000, 64, 32, 10, 100, 96
D = S + 3 * V
P = 128
NB = -(-N // P)
LAST = N - P
U = -(-E // (2 * P))
EP = U * 2 * P
UG = 17
UP = U // UG
C_S = math.sin(math.pi / 8.0)
C_X = math.cos(math.pi / 8.0)
AVG = 4.0
LN_CHUNK = 7
NCH = NB // LN_CHUNK
RING = 4
LAGS = 4
LAG = 2
AB, CD = 4 * S, 3 * V
SUMS = AB + 2 * CD


def gnn_kernel(nc, x, dst_u, dst_t, src_t, attr_t, len_T, nv, w, out):
    assert UP * UG == U and NCH * LN_CHUNK == NB
    x1 = nc.dram_tensor("x1_table", (N, D), fp32).ap()
    tmm = nc.dram_tensor("pair_min_max", (2, U), fp32).ap()
    rng = nc.dram_tensor("window_ranges", (NB, 4), i32).ap()

    ctx = ExitStack()
    with ctx:
        def sb(name, shape, dt=fp32):
            return ctx.enter_context(nc.sbuf_tensor(name, shape, dt))

        def sem(name):
            return ctx.enter_context(nc.semaphore(name))

        bank = [ctx.enter_context(nc.psum_tensor(f"bank{i}", [P, 512], fp32)) for i in range(8)]

        base = sb("base", [P, NB, D])
        xc = sb("xc", [P, NB, D])
        stat = sb("stat", [P, 2, 4, LN_CHUNK])
        rstd = sb("rstd", [P, NB])
        nvs = sb("nvs", [P, 3, NB])
        arcr = sb("arcr", [P, 2, NB])
        uauc = sb("uauc", [P, 2, NB])
        xs = sb("xs", [P, 2, 2 * D])
        hT = sb("hT", [P, 2, 3 * P])
        wn = sb("wn", [P, 2 * D])
        wl2 = sb("wl2", [MID, 4, MID])
        wl3s = sb("wl3s", [MID, S])
        wl3v = sb("wl3v", [MID, V])
        fold = sb("fold", [MID, 2 * S + 2 * V])
        wfc1 = sb("wfc1", [NBAS, H])
        wfc2 = sb("wfc2", [H, 2 * MID])
        src = sb("src", [P, 2 * U], i32)
        dstf = sb("dstf", [P, 2 * U])
        attr = sb("attr", [P, 2 * U, 4])
        idx = sb("idx", [P, RING, 2], i32)
        lenr = sb("lenr", [NBAS, RING, 2 * P])
        work = sb("work", [P, RING * 2 * D + 2 * 4 * MID + 2 * SUMS])
        G = work[:, 0:RING * 2 * D].rearrange("p (r j f) -> p r j f", r=RING, j=2)
        wts = work[:, RING * 2 * D:RING * 2 * D + 2 * 4 * MID].rearrange("p (j c f) -> p j c f", j=2, c=4)
        prod = work[:, RING * 2 * D + 2 * 4 * MID:].rearrange("p (j f) -> p j f", j=2)
        sq = work[:, 0:2 * LN_CHUNK * D].rearrange("p (k f) -> p k f", k=2)
        hid = sb("hid", [H, 2, P])
        hot = sb("hot", [P, 2, P])
        agg = sb("agg", [P, 4, MID])
        aggT = sb("aggT", [MID, 4 * P])
        outs = sb("outs", [P, 2, D])
        zero = sb("zero", [1, 512], bf16)
        ident = sb("ident", [P, P])
        iota_i = sb("iota_i", [P, P], i32)
        iota_f = sb("iota_f", [P, P])
        iota_w = sb("iota_w", [P, P])
        part_f = sb("part_f", [P, 1])
        xflat = xc[:].rearrange("p w f -> p (w f)")
        o = UG * 2 * P
        dstu = xflat[0:UP, 0:o].bitcast(i32).rearrange("p (g e) -> p g e", g=UG)
        mmb = xflat[0:NB, o:o + 2 * U].rearrange("p (k u) -> p k u", k=2)
        pos_i = xflat[0:NB, o + 2 * U:o + 3 * U].bitcast(i32)
        pos = xflat[0:NB, o + 3 * U:o + 4 * U]
        dst_i = xflat[:, o + 4 * U:o + 6 * U].bitcast(i32)
        mm = sb("mm", [UP, 2, UG])
        wst = sb("wst", [P, NB])
        wst_c = sb("wst_c", [NB, 2])
        hl = sb("hl", [NB, 4])
        tri = sb("tri", [NB, NB])
        rngc = sb("rngc", [NB, 4], i32)
        row = sb("row", [1, NB * 4], i32)

        in_loaded = sem("in_loaded")
        x_loaded = sem("x_loaded")
        dstu_loaded = sem("dstu_loaded")
        zeroed = sem("zeroed")
        iotas = sem("iotas")
        consts = sem("consts")
        mm_done = sem("mm_done")
        mm_stored = sem("mm_stored")
        mm_loaded = sem("mm_loaded")
        cnt_done = sem("cnt_done")
        cum_done = sem("cum_done")
        rng_done = sem("rng_done")
        rng_stored = sem("rng_stored")
        row_loaded = sem("row_loaded")
        fold_mm = sem("fold_mm")
        fold_done = sem("fold_done")
        xc_ready = sem("xc_ready")
        sq_done = sem("sq_done")
        var_done = sem("var_done")
        std_done = sem("std_done")
        ln_done = sem("ln_done")
        xs_ready = sem("xs_ready")
        xs_free = sem("xs_free")
        h_t = sem("h_t")
        h_evac = sem("h_evac")
        n_mm = sem("n_mm")
        n_x1 = sem("n_x1")
        n_done = [sem(f"n_done{q}") for q in range(2)]
        wn_loaded = sem("wn_loaded")
        wn_scaled = sem("wn_scaled")
        x1_ready = sem("x1_ready")
        x1_stored = sem("x1_stored")
        idx_loaded = [sem(f"idx_loaded{k}") for k in range(RING)]
        idx_free = sem("idx_free")
        len_loaded = [sem(f"len_loaded{k}") for k in range(RING)]
        len_ready = sem("len_ready")
        len_free = sem("len_free")
        gathered = [sem(f"gathered{k}") for k in range(RING)]
        g_ready = sem("g_ready")
        g_free = sem("g_free")
        pre_ready = sem("pre_ready")
        hid_ready = [sem(f"hid_ready{j}") for j in range(2)]
        w_ready = [sem(f"w_ready{j}") for j in range(2)]
        wts_ready = [sem(f"wts_ready{j}") for j in range(2)]
        prod_ready = [sem(f"prod_ready{j}") for j in range(2)]
        prod_free = [sem(f"prod_free{j}") for j in range(2)]
        agg_free = sem("agg_free")
        agg_d = sem("agg_d")
        agg_copied = sem("agg_copied")
        aggT_mm = sem("aggT_mm")
        aggT_ready = sem("aggT_ready")
        o_mm = sem("o_mm")
        o_free = sem("o_free")
        out_ready = sem("out_ready")
        out_stored = [sem(f"out_stored{q}") for q in range(2)]

        def take(eng, s, n=1):
            eng.wait_ge(s, n).then_inc(s, -n)

        PAIRS = NB // 2
        loads = [
            (nvs[:], nv),
            (wfc1[:], w["W_fc1"]),
            (wfc2[:].rearrange("h (k f) -> h k f", k=2)[:, :, 0:S],
             w["W_fc2"][:, 0:2 * S].rearrange("h (k f) -> h k f", k=2)),
            (wfc2[:].rearrange("h (k f) -> h k f", k=2)[:, :, S:MID],
             w["W_fc2"][:, 2 * S:2 * MID].rearrange("h (k f) -> h k f", k=2)),
            (wl3s[:], w["Ws_l3"]), (wl3v[:], w["Wv_l3"]),
            (wl2[:, 0, :], w["Ws_l2_aT"]), (wl2[:, 1, :], w["Ws_l2_cT"]),
            (wl2[:, 2, :], w["Wv_l2_aT"]), (wl2[:, 3, :], w["Wv_l2_cT"]),
            (src[:], src_t), (dst_i, dst_t), (attr[:], attr_t),
        ]
        wn_loads = []
        blocks = wn[:].rearrange("p (k t u) -> p k t u", k=5, t=2)
        for t, step in enumerate(("l1", "sc")):
            for h, kind in enumerate("ac"):
                ws, wv = w[f"Ws_{step}_{kind}"], w[f"Wv_{step}_{kind}"]
                for k in range(2):
                    wn_loads += [(blocks[64 * k + 32 * h:64 * k + 32 * h + 32, 0:2, t, :],
                                  ws[32 * k:32 * k + 32, :].rearrange("p (k u) -> p k u", k=2)),
                                 (blocks[64 * k + 32 * h:64 * k + 32 * h + 32, 2 + k, t, :], wv)]
                wn_loads += [(blocks[32 * h:32 * h + 32, 4, t, :], wv)]
        N_LOADS = 16 * len(loads)

        def edge_range(eng, b):
            first = eng.value_load(row[0:1, bass.ds(b * 4, 1)], min_val=0, max_val=U - 1)
            count = eng.value_load(row[0:1, bass.ds(b * 4 + 1, 1)], min_val=1, max_val=U)
            before = eng.value_load(row[0:1, bass.ds(b * 4 + 2, 1)], min_val=0, max_val=NB * U)
            return first, count, before

        def all_pairs(eng):
            _, count, before = edge_range(eng, NB - 1)
            return count + before

        def windows(eng, window, end):
            for b in range(LAGS):
                window(b, b % 2)
                end(b, b % 2, range(1, b + 1))
            with eng.Fori(LAGS // 2, PAIRS) as p:
                for q in range(2):
                    window(p * 2 + q, q)
                    end(p * 2 + q, q, range(1, LAGS + 1))
            for b in range(NB, NB + LAGS):
                end(b, b % 2, range(b - NB + 1, LAGS + 1))

        block = ctx.enter_context(nc.Block())

        @block.sync
        def _(sp):
            sp.dma_start(dstu, dst_u).then_inc(dstu_loaded, 16)
            whole = x[0:(NB - 1) * P, :].rearrange("(w p) f -> p w f", p=P)
            for ch in range(NCH):
                a, z = ch * LN_CHUNK, min((ch + 1) * LN_CHUNK, NB - 1)
                sp.dma_start(base[:, a:z, :], whole[:, a:z, :]).then_inc(x_loaded, 16)
            sp.dma_start(base[:, NB - 1, :], x[LAST:N, :]).then_inc(x_loaded, 16)
            sp.wait_ge(zeroed, 1)
            for to, fr in wn_loads:
                sp.dma_start(to, fr).then_inc(wn_loaded, 16)
            for to, fr in loads:
                sp.dma_start(to, fr).then_inc(in_loaded, 16)
            sp.wait_ge(mm_done, 1)
            for k in range(2):
                sp.dma_start(tmm[k].rearrange("(p g) -> p g", g=UG), mm[:, k, :]).then_inc(mm_stored, 16)
            sp.wait_ge(mm_stored, 32)
            sp.dma_start(mmb, tmm.unsqueeze(0).to_broadcast([NB, 2, U])).then_inc(mm_loaded, 16)
            sp.wait_ge(rng_done, 1)
            sp.dma_start(rng, rngc[:]).then_inc(rng_stored, 16)
            sp.wait_ge(rng_stored, 16)
            sp.dma_start(row[:], rng.rearrange("b k -> (b k)").unsqueeze(0)).then_inc(row_loaded, 16)
            for ch in range(NCH):
                a, z = ch * LN_CHUNK, min((ch + 1) * LN_CHUNK, NB - 1)
                sp.wait_ge(x1_ready, (z - a) + a)
                sp.dma_start(x1[0:(NB - 1) * P, :].rearrange("(w p) f -> p w f", p=P)[:, a:z, :],
                             xc[:, a:z, :]).then_inc(x1_stored, 16)
            sp.wait_ge(x1_ready, NB)
            sp.wait_ge(x1_stored, 16 * NCH)
            sp.dma_start(x1[LAST:N, :], xc[:, NB - 1, :]).then_inc(x1_stored, 16)

            sp.wait_ge(row_loaded, 16)
            sp.wait_ge(in_loaded, N_LOADS)

            def issue(k, u):
                sp.dma_start(idx[:, k, :], src[:, bass.ds(u * 2, 2)]).then_inc(idx_loaded[k], 16)
                sp.dma_start(lenr[:, k, :], len_T[:, bass.ds(u * 2 * P, 2 * P)]).then_inc(len_loaded[k], 16)
                take(sp, len_loaded[(k - 1) % RING], 16)
                sp.sem_inc(len_ready, 1)

            def load_pair(step, u):
                take(sp, idx_free)
                take(sp, len_free)
                slot = sp.snap(step & (RING - 1))
                with sp.If(slot < 2):
                    with sp.If(slot < 1):
                        issue(0, u)
                    with sp.Else():
                        issue(1, u)
                    sp.nop()
                with sp.Else():
                    with sp.If(slot < 3):
                        issue(2, u)
                    with sp.Else():
                        issue(3, u)
                    sp.nop()

            sp.sem_inc(len_loaded[RING - 1], 16)
            sp.sem_inc(idx_free, RING)
            sp.sem_inc(len_free, RING)
            with sp.Fori(0, NB) as b:
                first, count, before = edge_range(sp, b)
                with sp.Fori(0, count) as i:
                    load_pair(before + i, (first + i).with_bounds(min_val=0, max_val=U - 1))
            total = all_pairs(sp)
            with sp.Fori(0, sp.snap((((total + RING + 1) >> 2) << 2) - total)) as i:
                load_pair(total + i, i.with_bounds(min_val=0, max_val=RING + 1))
            take(sp, len_loaded[RING - 1], 16)
            sp.sem_inc(len_ready, 1)

        @block.gpsimd
        def _(pool):
            nc.gpsimd.memset(wn[:], 0.0).then_inc(zeroed, 1)
            nc.gpsimd.iota(iota_i[:], [[1, P]], base=0, channel_multiplier=0).then_inc(iotas, 1)
            nc.gpsimd.iota(pos_i, [[1, U]], base=0, channel_multiplier=0).then_inc(iotas, 1)
            nc.gpsimd.memset(ident[:], 0.0).then_inc(iotas, 1)
            pool.wait_ge(iotas, 3)
            nc.gpsimd.affine_select(out=ident[:], in_=ident[:], compare_op=ALU.not_equal, fill=1.0, base=0,
                                    pattern=[[-1, P]], channel_multiplier=1).then_inc(consts, 1)
            nc.gpsimd.memset(tri[:], 1.0).then_inc(iotas, 1)
            pool.wait_ge(iotas, 4)
            nc.gpsimd.affine_select(out=tri[:], in_=tri[:], compare_op=ALU.is_gt, fill=0.0, base=0,
                                    pattern=[[1, NB]], channel_multiplier=-1).then_inc(consts, 1)
            nc.gpsimd.memset(zero[:], 0.0).then_inc(consts, 1)

            pool.wait_ge(row_loaded, 16)
            rounds = pool.snap((all_pairs(pool) + RING + 1) >> 2)
            pool.wait_ge(x1_stored, 16 * (NCH + 1))

            def round_(g):
                for k in range(RING):
                    take(pool, idx_loaded[k], 16)
                    take(pool, g_free)
                    for j in range(2):
                        pool.indirect_dma_start(
                            out=G[:, k, j, :], out_offset=None, in_=x1,
                            in_offset=bass.IndirectOffsetOnAxis(ap=idx[:, k, j:j + 1], axis=0),
                        ).then_inc(gathered[k], 16)
                    if k >= LAG:
                        pool.wait_ge(gathered[k - LAG], g * 32 + 32).then_inc(g_ready, 1)
                        pool.sem_inc(idx_free, 1)
                    elif not isinstance(g, int):
                        pool.wait_ge(gathered[k - LAG + RING], g * 32).then_inc(g_ready, 1)
                        pool.sem_inc(idx_free, 1)

            round_(0)
            with pool.Fori(1, rounds) as g:
                round_(g)
            for k in range(RING - LAG, RING):
                pool.wait_ge(gathered[k], rounds * 32).then_inc(g_ready, 1)
                pool.sem_inc(idx_free, 1)

        @block.scalar
        def _(act):
            for ch in range(NCH):
                a = ch * LN_CHUNK
                act.wait_ge(xc_ready, ch + 1)
                if ch >= 2:
                    act.wait_ge(var_done, ch - 1)
                nc.scalar.activation(sq[:, ch % 2].rearrange("p (w f) -> p w f", w=LN_CHUNK),
                                     xc[:, a:a + LN_CHUNK, :], ACT.Square).then_inc(sq_done, 1)
                if ch >= 1:
                    act.wait_ge(var_done, ch)
                    nc.scalar.activation(stat[:, (ch - 1) % 2, 3, :], stat[:, (ch - 1) % 2, 2, :],
                                         ACT.Sqrt).then_inc(std_done, 1)
            act.wait_ge(var_done, NCH)
            nc.scalar.activation(stat[:, (NCH - 1) % 2, 3, :], stat[:, (NCH - 1) % 2, 2, :],
                                 ACT.Sqrt).then_inc(std_done, 1)

            act.wait_ge(ln_done, 1)
            with act.Fori(0, PAIRS) as p:
                for q in range(2):
                    take(act, h_t)
                    act.sem_inc(xs_free, 1)
                    nc.scalar.copy(hT[:, q, 0:2 * P], bank[q][:, 0:2 * P])
                    nc.scalar.copy(hT[0:2 * V, q, 2 * P:3 * P], bank[q][0:2 * V, 2 * P:3 * P]).then_inc(h_evac, 1)
                for q in range(2):
                    take(act, n_mm)
                    nc.scalar.copy(xc[:, bass.ds(p * 2 + q, 1), :].rearrange("p o (k u) -> p (o k) u", k=5),
                                   bank[2 + q][:, 0:2 * D].rearrange("p (k t u) -> p k t u", k=5, t=2)[:, :, 0, :]
                                   ).then_inc(n_x1, 1)

            act.wait_ge(fold_mm, 1)
            nc.scalar.activation(fold[0:64, 0:128], bank[6][0:64, 0:128], ACT.Copy)
            nc.scalar.activation(fold[64:96, 0:128], bank[6][64:96, 0:128], ACT.Copy, scale=1.0 / math.sqrt(3.0))
            nc.scalar.activation(fold[:, 128:192], bank[6][0:96, 128:192], ACT.Copy).then_inc(fold_done, 1)

            act.wait_ge(row_loaded, 16)

            def silu(j):
                if j == 0:
                    take(act, pre_ready)
                    act.sem_inc(len_free, 1)
                nc.scalar.activation(hid[:, j, :], bank[0][0:H, P * j:P * (j + 1)], ACT.Silu
                                     ).then_inc(hid_ready[j], 1)

            def window(b, q):
                first, count, before = edge_range(act, b)
                with act.Fori(0, count) as i:
                    u2 = (first + i).with_bounds(min_val=0, max_val=U - 1) * 2
                    for j in range(2):
                        take(act, w_ready[j])
                        for c in range(4):
                            last = nc.scalar.activation(wts[:, j, c, :],
                                                        bank[1 + j][:, MID * (c > 0):MID * (c > 0) + MID], ACT.Copy,
                                                        scale=attr[:, bass.ds(u2 + j, 1), c])
                        last.then_inc(wts_ready[j], 1)
                        silu(j)

            def end(b, q, lags):
                if 4 in lags:
                    take(act, out_ready)
                    act.sem_inc(o_free, 1)
                    if isinstance(b, int) and b - 4 == NB - 1:
                        act.wait_ge(out_stored[1 - q], 16)
                    start = act.value_load(row[0:1, bass.ds(b * 4 - 13, 1)], min_val=0, max_val=LAST)
                    act.dma_start(out[bass.ds(start, P), :], outs[:, q, :]).then_inc(out_stored[q], 16)
                if 2 in lags:
                    take(act, aggT_mm)
                    nc.scalar.copy(aggT[:], bank[4][0:MID, :]).then_inc(aggT_ready, 1)
                if 1 in lags:
                    take(act, agg_d)
                    sums = bank[3 + 3 * (1 - q)]
                    nc.scalar.copy(agg[:, :, 0:S], sums[:, 0:AB].rearrange("p (k f) -> p k f", k=4))
                    nc.scalar.copy(agg[:, 1:4, S:MID], sums[:, AB:AB + CD].rearrange("p (c u) -> p c u", c=3)
                                   ).then_inc(agg_copied, 1)

            silu(0)
            silu(1)
            windows(act, window, end)

        @block.vector
        def _(dve):
            dve.wait_ge(iotas, 2)
            nc.vector.tensor_copy(iota_f[:], iota_i[:])
            nc.vector.tensor_copy(pos, pos_i)
            dve.wait_ge(dstu_loaded, 16)
            nc.vector.tensor_reduce(mm[:, 0, :], dstu, AX.X, ALU.min)
            nc.vector.tensor_reduce(mm[:, 1, :], dstu, AX.X, ALU.max).then_inc(mm_done, 1)
            dve.drain()
            nc.vector.tensor_scalar(wst[:], iota_f[:, 0:NB], float(P), float(LAST), ALU.mult, ALU.min)
            dve.wait_ge(consts, 1)
            nc.vector.tensor_tensor(iota_w[:], iota_f[:], ident[:], ALU.mult)
            dve.drain()
            nc.vector.reduce_sum(part_f[:], iota_w[:], axis=AX.X)
            dve.drain()
            nc.vector.tensor_scalar(wst_c[:, 0:1], part_f[0:NB, :], float(P), float(LAST), ALU.mult, ALU.min)
            dve.drain()
            nc.vector.tensor_scalar(wst_c[:, 1:2], wst_c[:, 0:1], float(P), None, ALU.add)
            dve.wait_ge(mm_loaded, 16)
            dve.drain()
            lo, hi = mmb[:, 0, :], mmb[:, 1, :]
            nc.vector.tensor_scalar(lo, lo, wst_c[:, 1:2], None, ALU.is_lt)
            dve.drain()
            nc.vector.scalar_tensor_tensor(out=lo, in0=hi, scalar=wst_c[:, 0:1], in1=lo, op0=ALU.is_ge, op1=ALU.mult)
            dve.drain()
            nc.vector.scalar_tensor_tensor(out=hi, in0=pos, scalar=1.0, in1=lo, op0=ALU.add, op1=ALU.mult)
            dve.drain()
            nc.vector.reduce_max(hl[:, 0:1], hi, axis=AX.X)
            dve.drain()
            nc.vector.tensor_scalar(pos, pos, -1.0, float(U), ALU.mult, ALU.add)
            dve.drain()
            nc.vector.tensor_tensor(hi, pos, lo, ALU.mult)
            dve.drain()
            nc.vector.reduce_max(hl[:, 1:2], hi, axis=AX.X)
            dve.drain()
            nc.vector.tensor_scalar(hl[:, 0:1], hl[:, 0:1], 1.0, None, ALU.max)
            nc.vector.tensor_scalar(hl[:, 1:2], hl[:, 1:2], -1.0, float(U), ALU.mult, ALU.add)
            dve.drain()
            nc.vector.tensor_scalar(hl[:, 2:3], hl[:, 0:1], 1.0, None, ALU.subtract)
            dve.drain()
            nc.vector.tensor_tensor(hl[:, 1:2], hl[:, 1:2], hl[:, 2:3], ALU.min)
            dve.drain()
            nc.vector.tensor_tensor(hl[:, 2:3], hl[:, 0:1], hl[:, 1:2], ALU.subtract).then_inc(cnt_done, 1)
            dve.wait_ge(cum_done, 1)
            nc.vector.tensor_copy(rngc[:, 0:1], hl[:, 1:2])
            dve.drain()
            nc.vector.tensor_copy(rngc[:, 1:2], hl[:, 2:3])
            nc.vector.tensor_copy(rngc[:, 3:4], wst_c[:, 0:1])
            nc.vector.tensor_copy(rngc[:, 2:3], bank[7][0:NB, 0:1]).then_inc(rng_done, 1)

            dve.wait_ge(in_loaded, N_LOADS)
            nc.vector.tensor_copy(dstf[:], dst_i)
            dve.drain()

            def variance(ch):
                st = stat[:, ch % 2]
                dve.wait_ge(sq_done, ch + 1)
                nc.vector.reduce_sum(st[:, 0, :], sq[:, ch % 2].rearrange("p (w f) -> p w f", w=LN_CHUNK),
                                     axis=AX.X)
                dve.drain()
                nc.vector.tensor_scalar(st[:, 2, :], st[:, 0, :], 1.0 / D, 1e-5, ALU.mult,
                                        ALU.add).then_inc(var_done, 1)

            def inverse(ch):
                dve.wait_ge(std_done, ch + 1)
                nc.vector.reciprocal(rstd[:, ch * LN_CHUNK:(ch + 1) * LN_CHUNK], stat[:, ch % 2, 3, :])

            for ch in range(NCH):
                a = ch * LN_CHUNK
                z = a + LN_CHUNK
                dve.wait_ge(x_loaded, 16 * (NCH + 1))
                if ch >= 2:
                    inverse(ch - 2)
                    dve.drain()
                st = stat[:, ch % 2]
                nc.vector.reduce_sum(st[:, 0, :], base[:, a:z, :], axis=AX.X)
                dve.drain()
                nc.vector.tensor_scalar(st[:, 1, :], st[:, 0, :], 1.0 / D, None, ALU.mult)
                dve.drain()
                mean = st[:, 1, :]
                nc.vector.tensor_tensor(xc[:, a:z, 0:S], base[:, a:z, 0:S],
                                        mean.unsqueeze(2).to_broadcast([P, LN_CHUNK, S]), ALU.subtract)
                nc.vector.tensor_tensor(xc[:, a:z, S:D].rearrange("p w (c u) -> p w c u", c=3),
                                        base[:, a:z, S:D].rearrange("p w (u c) -> p w c u", c=3),
                                        mean.unsqueeze(2).unsqueeze(3).to_broadcast([P, LN_CHUNK, 3, V]),
                                        ALU.subtract).then_inc(xc_ready, 1)
                if ch >= 1:
                    variance(ch - 1)
            variance(NCH - 1)
            inverse(NCH - 2)
            inverse(NCH - 1)
            dve.drain()
            for k in range(2):
                nc.vector.tensor_tensor(arcr[:, k, :], nvs[:, k, :], rstd[:], ALU.mult)
                nc.vector.scalar_tensor_tensor(out=uauc[:, k, :], in0=nvs[:, k, :], scalar=C_X / AVG,
                                               in1=nvs[:, 2, :], op0=ALU.mult, op1=ALU.mult)
            dve.wait_ge(wn_loaded, 16 * len(wn_loads))
            nc.vector.tensor_scalar(blocks[:, :, 1, :], blocks[:, :, 1, :], C_S, None, ALU.mult).then_inc(wn_scaled, 1)
            dve.drain().then_inc(ln_done, 1)

            def node_input(p):
                for q in range(2):
                    take(dve, xs_free)
                    for k in range(2):
                        last = nc.vector.tensor_scalar(
                            xs[:, q, :].rearrange("p (k t u) -> p k t u", k=5, t=2)[:, :, k, :],
                            xc[:, bass.ds(p * 2 + q, 1), :].rearrange("p o (k u) -> p (o k) u", k=5),
                            0.0, arcr[:, k, bass.ds(p * 2 + q, 1)], ALU.max, ALU.mult)
                    last.then_inc(xs_ready, 1)

            def node_output(p):
                for q in range(2):
                    take(dve, n_x1)
                    dve.sem_inc(x1_ready, 1)
                    sc = bank[2 + q][:, 0:2 * D].rearrange("p (k t u) -> p k t u", k=5, t=2)[:, :, 1, :]
                    bw = base[:, bass.ds(p * 2 + q, 1), :].rearrange("p o f -> p (o f)")
                    bs = bw[:, 0:S].rearrange("p (k u) -> p k u", k=2)
                    nc.vector.tensor_tensor(bs, bs, sc[:, 0:2], ALU.add)
                    bv = bw[:, S:D].rearrange("p (u c) -> p c u", c=3)
                    nc.vector.tensor_tensor(bv, bv, sc[:, 2:5], ALU.add).then_inc(n_done[q], 1)

            dve.sem_inc(xs_free, 2)
            node_input(0)
            with dve.Fori(1, PAIRS) as p:
                node_input(p)
                node_output(p - 1)
            node_output(PAIRS - 1)

            dve.wait_ge(row_loaded, 16)
            for j in range(2):
                dve.sem_inc(prod_free[j], 1)
                dve.sem_inc(out_stored[j], 16)
            dve.sem_inc(agg_free, 1)
            dve.sem_inc(g_free, RING)
            dve.sem_inc(o_free, 2)
            dve.drain()

            def window(b, q):
                first, count, before = edge_range(dve, b)
                dve.drain()
                nc.vector.tensor_scalar(iota_w[:], iota_f[:], wst[:, bass.ds(b, 1)], None, ALU.add)
                dve.drain()
                with dve.Fori(0, count) as i:
                    u2 = (first + i).with_bounds(min_val=0, max_val=U - 1) * 2
                    slot = dve.snap((before + i) & (RING - 1))
                    for j in range(2):
                        take(dve, prod_free[j])
                        nc.vector.tensor_scalar(hot[:, j, :], iota_w[:], dstf[:, bass.ds(u2 + j, 1)], None,
                                                ALU.is_equal)
                        if j == 0:
                            take(dve, g_ready)
                        take(dve, wts_ready[j])
                        g = G[:, bass.ds(slot, 1), j, :].rearrange("p o f -> p (o f)")
                        gv = g[:, S:D].rearrange("p (c u) -> p c u", c=3)
                        nc.vector.tensor_tensor(prod[:, j, 0:AB].rearrange("p (k f) -> p k f", k=4),
                                                wts[:, j, :, 0:S], g[:, 0:S].unsqueeze(1).to_broadcast([P, 4, S]),
                                                ALU.mult)
                        nc.vector.tensor_tensor(prod[:, j, AB:AB + CD].rearrange("p (c u) -> p c u", c=3), gv,
                                                wts[:, j, 0:1, S:MID].to_broadcast([P, 3, V]), ALU.mult)
                        nc.vector.tensor_tensor(prod[:, j, AB + CD:SUMS].rearrange("p (c u) -> p c u", c=3), gv,
                                                wts[:, j, 1:4, S:MID], ALU.mult).then_inc(prod_ready[j], 1)

            def end(b, q, lags):
                if 1 in lags:
                    if isinstance(b, int) and b == NB:
                        dve.wait_ge(prod_free[1], 1)
                    take(dve, agg_free)
                    sums = bank[3 + 3 * (1 - q)]
                    nc.vector.tensor_reduce(agg[:, 0, S:MID], sums[:, AB + CD:SUMS].rearrange("p (c u) -> p u c", c=3),
                                            AX.X, ALU.add).then_inc(agg_d, 1)
                if 3 in lags:
                    take(dve, out_stored[1 - q], 16)
                    take(dve, o_mm)
                    o = bank[5 + 2 * (1 - q)]
                    to = outs[:, 1 - q, :]
                    bw = base[:, bass.ds(b - 3, 1), :].rearrange("p o f -> p (o f)")
                    ua, uc = uauc[:, 0, bass.ds(b - 3, 1)], uauc[:, 1, bass.ds(b - 3, 1)]
                    ov = to[:, S:D].rearrange("p (u c) -> p c u", c=3)
                    pv = o[:, 128:320].rearrange("p (c k u) -> p c k u", c=3, k=2)

                    def stt(to, in0, scalar, in1):
                        return nc.vector.scalar_tensor_tensor(out=to, in0=in0, scalar=scalar, in1=in1, op0=ALU.mult,
                                                              op1=ALU.add)
                    stt(to[:, 0:S], o[:, 0:64], ua, bw[:, 0:S])
                    stt(ov, pv[:, :, 0, :], ua, bw[:, S:D].rearrange("p (u c) -> p c u", c=3))
                    dve.drain()
                    stt(to[:, 0:S], o[:, 64:128], uc, to[:, 0:S])
                    stt(ov, pv[:, :, 1, :], uc, ov).then_inc(out_ready, 1)

            windows(dve, window, end)
            take(dve, out_stored[(NB - 1) % 2], 16)
            take(dve, out_stored[NB % 2], 16)

        @block.tensor
        def _(pe):
            pe.wait_ge(cnt_done, 1)
            pe.wait_ge(consts, 3)
            nc.tensor.matmul(bank[7][0:NB, 0:1], tri[:], hl[:, 2:3], start=True, stop=True).then_inc(cum_done, 1)
            pe.wait_ge(in_loaded, N_LOADS)
            for k in range(2):
                nc.tensor.matmul(bank[6][0:MID, S * k:S * (k + 1)], wl2[:, k, :], wl3s[:], start=True, stop=True)
            for k in range(2):
                last = nc.tensor.matmul(bank[6][0:MID, 128 + V * k:128 + V * (k + 1)], wl2[:, 2 + k, :], wl3v[:],
                                        start=True, stop=True)
            last.then_inc(fold_mm, 1)

            pe.wait_ge(ln_done, 1)
            pe.wait_ge(wn_scaled, 1)
            for q in range(2):
                pe.sem_inc(n_done[q], 1)
            with pe.Fori(0, PAIRS) as p:
                for q in range(2):
                    take(pe, xs_ready)
                    for k in range(2):
                        nc.tensor.transpose(bank[q][:, P * k:P * (k + 1)], xs[:, q, P * k:P * (k + 1)], ident[:])
                    nc.tensor.transpose(bank[q][0:2 * V, 2 * P:3 * P], xs[:, q, 2 * P:2 * D], ident[:]
                                        ).then_inc(h_t, 1)
                for q in range(2):
                    take(pe, h_evac)
                    take(pe, n_done[q])
                    for k in range(2):
                        nc.tensor.matmul(bank[2 + q][:, P * k:P * (k + 1)], hT[:, q, P * k:P * (k + 1)],
                                         wn[:, P * k:P * (k + 1)], start=True, stop=True, skip_group_check=True)
                    nc.tensor.matmul(bank[2 + q][:, 2 * P:2 * D], hT[0:2 * V, q, 2 * P:3 * P],
                                     wn[0:2 * V, 2 * P:2 * D], start=True, stop=True,
                                     skip_group_check=True).then_inc(n_mm, 1)
            for q in range(2):
                take(pe, n_done[q])

            def first_map(step):
                take(pe, len_ready)
                slot = pe.snap(step & (RING - 1))
                nc.tensor.matmul(bank[0][0:H, 0:2 * P], wfc1[:],
                                 lenr[:, bass.ds(slot, 1), :].rearrange("p o e -> p (o e)"),
                                 start=True, stop=True).then_inc(pre_ready, 1)

            def second_map(j):
                take(pe, hid_ready[j])
                nc.tensor.matmul(bank[1 + j][:, 0:2 * MID], hid[:, j, :], wfc2[:], start=True,
                                 stop=True).then_inc(w_ready[j], 1)

            def window(b, q):
                first, count, before = edge_range(pe, b)
                sums = bank[3 + 3 * q][:, 0:SUMS]
                nc.tensor.matmul(sums, zero[:, 0:P], zero[:, 0:SUMS], start=True, stop=False,
                                 skip_group_check=True)
                with pe.Fori(0, count) as i:
                    for j in range(2):
                        take(pe, prod_ready[j])
                        if j == 1:
                            pe.sem_inc(g_free, 1)
                        second_map(j)
                        if j == 1:
                            first_map(before + i + 2)
                        nc.tensor.matmul(sums, hot[:, j, :], prod[:, j, :], start=False, stop=(j == 1),
                                         skip_group_check=True).then_inc(prod_free[j], 1)

            def end(b, q, lags):
                if 2 in lags:
                    take(pe, aggT_ready)
                    take(pe, o_free)
                    o = bank[5 + 2 * q]
                    nc.tensor.matmul(o[:, 0:128], aggT[:, 0:P], fold[:, 0:128], start=True, stop=True,
                                     skip_group_check=True)
                    for c in range(3):
                        last = nc.tensor.matmul(o[:, 128 + 64 * c:192 + 64 * c], aggT[:, P * (c + 1):P * (c + 2)],
                                                fold[:, 128:192], start=True, stop=True, skip_group_check=True)
                    last.then_inc(o_mm, 1)
                if 1 in lags:
                    take(pe, agg_copied)
                    nc.tensor.transpose(bank[4][0:MID, 0:P], agg[:, 0, :], ident[:]).then_inc(agg_free, 1)
                    for k in range(1, 4):
                        last = nc.tensor.transpose(bank[4][0:MID, P * k:P * (k + 1)], agg[:, k, :], ident[:])
                    last.then_inc(aggT_mm, 1)

            pe.wait_ge(fold_done, 1)
            take(pe, len_ready)
            first_map(0)
            second_map(0)
            second_map(1)
            first_map(1)
            windows(pe, window, end)
            pe.sem_inc(g_free, 1)


def kernel(**inputs):
    import numpy as np
    import concourse.bacc as bacc
    from concourse.bass_utils import run_bass_kernel_spmd as run

    a = {k: np.asarray(v) for k, v in inputs.items()}

    def edges(v):
        return np.pad(v, [(0, EP - E)] + [(0, 0)] * (v.ndim - 1), mode="edge")

    def lanes(v):
        v = v.reshape(2 * U, P, *v.shape[1:])
        return np.swapaxes(v, 0, 1)

    def windows(v):
        return np.concatenate([v[:(NB - 1) * P, 0].reshape(NB - 1, P).T, v[LAST:]], axis=1)

    arrays = {
        "x": a["x"],
        "dst_u": edges(a["dst"]).reshape(UP, UG, 2 * P),
        "dst_t": lanes(edges(a["dst"])),
        "src_t": lanes(edges(a["src"])),
        "attr_t": lanes(np.pad(a["edge_attr_4"], [(0, EP - E), (0, 0)])),
        "len_T": edges(a["edge_attr_10"]).T,
        "nv": np.stack([windows(a[k]) for k in ("node_vec1", "node_vec1_n2", "node_vec1_n3")], axis=1),
    }
    weights = {}
    for k, v in a.items():
        if k.startswith("L0_gnn_"):
            k = k[len("L0_gnn_"):]
            if "_l2_" in k:
                k, v = k + "T", v.T
            weights[k] = v
    nc = bacc.Bacc("TRN2", target_bir_lowering=False, num_devices=1)
    feed = {}

    def dram(name, v):
        v = np.ascontiguousarray(v)
        feed["in_" + name] = v
        return nc.dram_tensor("in_" + name, v.shape, mybir.dt.from_np(v.dtype), kind="ExternalInput").ap()

    args = {k: dram(k, v) for k, v in arrays.items()}
    w = {k: dram(k, v) for k, v in weights.items()}
    out = nc.dram_tensor("out", (N, D), fp32, kind="ExternalOutput").ap()
    gnn_kernel(nc, **args, w=w, out=out)
    return run(nc, [feed], core_ids=[0]).results[0]["out"]
```

```python
import concourse.bass as bass
from concourse import mybir
from contextlib import ExitStack
import math

fp32 = mybir.dt.float32
bf16 = mybir.dt.bfloat16
i32 = mybir.dt.int32
ALU = mybir.AluOpType
ACT = mybir.ActivationFunctionType
AX = mybir.AxisListType

N, E, S, V, NBAS, H, MID = 12500, 200000, 64, 32, 10, 100, 96
D = S + 3 * V
P = 128
NB = -(-N // P)
LAST = N - P
U = -(-E // (2 * P))
EP = U * 2 * P
UG = 17
UP = U // UG
C_S = math.sin(math.pi / 8.0)
C_X = math.cos(math.pi / 8.0)
AVG = 4.0
LN_CHUNK = 7
NCH = NB // LN_CHUNK
EARLY = 5
RB = 10
RING_LOG = 2
RING = 1 << RING_LOG
LAGS = 4
BUFS = 3
AHEAD = 2
LAG = 2
AB, CD = 4 * S, 3 * V
SUMS = AB + CD + V


def gnn_kernel(nc, x, dst_u, dst_t, src_p, attr_t, len_T, nv, w, out):
    assert UP * UG == U and NCH * LN_CHUNK == NB and U < 1 << RB and U << RB < 1 << 2 * RB
    x1 = nc.dram_tensor("x1_table", (N, D), fp32).ap()
    tmm = nc.dram_tensor("pair_min_max", (2, U), fp32).ap()
    rng = nc.dram_tensor("window_ranges", (NB, 2), i32).ap()

    ctx = ExitStack()
    with ctx:
        def sb(name, shape, dt=fp32):
            return ctx.enter_context(nc.sbuf_tensor(name, shape, dt))

        def sem(name):
            return ctx.enter_context(nc.semaphore(name))

        bank = [ctx.enter_context(nc.psum_tensor(f"bank{i}", [P, 512], fp32)) for i in range(8)]

        base = sb("base", [P, NB, D])
        xc = sb("xc", [P, NB, D])
        stat = sb("stat", [P, 2, 4, LN_CHUNK])
        rstd = sb("rstd", [P, NB])
        nvs = sb("nvs", [P, 3, NB])
        arcr = sb("arcr", [P, 2, NB])
        uauc = sb("uauc", [P, 2, NB])
        wn = sb("wn", [P, 2 * D])
        wl2 = sb("wl2", [MID, 4, MID])
        wl3s = sb("wl3s", [MID, S])
        wl3v = sb("wl3v", [MID, V])
        fold = sb("fold", [MID, 2 * S + 2 * V])
        wfc1 = sb("wfc1", [NBAS, H])
        wfc2 = sb("wfc2", [H, 2 * MID])
        dstf = sb("dstf", [P, 2 * U])
        attr = sb("attr", [P, 2 * U, 4])
        idx = sb("idx", [P, RING, 2], i32)
        lenr = sb("lenr", [NBAS, RING, 2 * P])
        n_g, n_w, n_p = RING * 2 * D, BUFS * 2 * 4 * MID, BUFS * 2 * SUMS
        work = sb("work", [P, n_g + n_w + n_p])
        G = work[:, 0:n_g].rearrange("p (r j f) -> p r j f", r=RING, j=2)
        wts = work[:, n_g:n_g + n_w].rearrange("p (r j c f) -> p r j c f", r=BUFS, j=2, c=4)
        prod = work[:, n_g + n_w:].rearrange("p (r j f) -> p r j f", r=BUFS, j=2)
        sq = work[:, 0:2 * LN_CHUNK * D].rearrange("p (k f) -> p k f", k=2)
        xs = work[:, 2 * LN_CHUNK * D:2 * LN_CHUNK * D + 4 * D].rearrange("p (q f) -> p q f", q=2)
        hT = work[:, 2 * LN_CHUNK * D + 4 * D:2 * LN_CHUNK * D + 4 * D + 6 * P].rearrange("p (q f) -> p q f", q=2)
        hid = sb("hid", [H, 2, P])
        dot = sb("dot", [P, BUFS, 2, CD])
        hot = sb("hot", [P, BUFS, 2, P])
        agg = sb("agg", [P, 4, MID])
        aggT = sb("aggT", [MID, 4 * P])
        outs = sb("outs", [P, 2, D])
        zero = sb("zero", [1, P], bf16)
        ident = sb("ident", [P, P])
        iota_i = sb("iota_i", [P, P], i32)
        iota_f = sb("iota_f", [P, P])
        iota_w = sb("iota_w", [P, 2, P])
        part_f = sb("part_f", [P, 1])
        xflat = xc[:].rearrange("p w f -> p (w f)")
        assert (UG * 2 * P + 6 * U) <= (NB - EARLY * LN_CHUNK) * D
        xflat = xflat[:, EARLY * LN_CHUNK * D:]
        o = UG * 2 * P
        dstu = xflat[0:UP, 0:o].bitcast(i32).rearrange("p (g e) -> p g e", g=UG)
        mmb = xflat[0:NB, o:o + 2 * U].rearrange("p (k u) -> p k u", k=2)
        pos_i = xflat[0:NB, o + 2 * U:o + 3 * U].bitcast(i32)
        pos = xflat[0:NB, o + 3 * U:o + 4 * U]
        dst_i = xflat[:, o + 4 * U:o + 6 * U].bitcast(i32)
        mm = sb("mm", [UP, 2, UG])
        wst = sb("wst", [P, NB + 1])
        wst_c = sb("wst_c", [NB, 2])
        hl = sb("hl", [NB, 4])
        tri = sb("tri", [NB, NB])
        rngc = sb("rngc", [NB, 2], i32)
        phase = sb("phase", [NB, 1], i32)
        row = sb("row", [1, (NB + 1) * 2], i32)

        in_loaded = sem("in_loaded")
        x_loaded = [sem(f"x_loaded{ch}") for ch in range(NCH)]
        dstu_loaded = sem("dstu_loaded")
        zeroed = sem("zeroed")
        iotas = sem("iotas")
        consts = sem("consts")
        mm_done = sem("mm_done")
        mm_stored = sem("mm_stored")
        mm_loaded = sem("mm_loaded")
        cnt_done = sem("cnt_done")
        cum_done = sem("cum_done")
        rng_done = sem("rng_done")
        rng_stored = sem("rng_stored")
        row_loaded = sem("row_loaded")
        fold_mm = sem("fold_mm")
        fold_done = sem("fold_done")
        xc_ready = sem("xc_ready")
        sq_done = sem("sq_done")
        relu_done = sem("relu_done")
        var_done = sem("var_done")
        std_done = sem("std_done")
        ln_done = sem("ln_done")
        xs_ready = sem("xs_ready")
        xs_free = sem("xs_free")
        h_t = sem("h_t")
        h_evac = sem("h_evac")
        n_mm = sem("n_mm")
        n_x1 = sem("n_x1")
        n_done = [sem(f"n_done{q}") for q in range(2)]
        wn_loaded = sem("wn_loaded")
        wn_scaled = sem("wn_scaled")
        x1_ready = sem("x1_ready")
        x1_stored = sem("x1_stored")
        loaded = [sem(f"loaded{way}") for way in range(3)]
        idx_ready = sem("idx_ready")
        idx_free = sem("idx_free")
        len_ready = sem("len_ready")
        len_free = sem("len_free")
        gathered = [sem(f"gathered{k}") for k in range(RING)]
        g_ready = sem("g_ready")
        g_free = sem("g_free")
        pre_ready = [sem(f"pre_ready{j}") for j in range(2)]
        hid_ready = [sem(f"hid_ready{j}") for j in range(2)]
        w_ready = [sem(f"w_ready{j}") for j in range(2)]
        wts_ready = [sem(f"wts_ready{r}") for r in range(BUFS)]
        wts_free = [sem(f"wts_free{r}") for r in range(BUFS)]
        prod_ready = [sem(f"prod_ready{r}") for r in range(BUFS)]
        prod_free = [sem(f"prod_free{r}") for r in range(BUFS)]
        dot_done = sem("dot_done")
        sums_done = sem("sums_done")
        agg_copied = sem("agg_copied")
        aggT_mm = sem("aggT_mm")
        aggT_ready = sem("aggT_ready")
        o_mm = sem("o_mm")
        o_ready = sem("o_ready")
        o_free = sem("o_free")
        out_ready = sem("out_ready")
        out_stored = [sem(f"out_stored{q}") for q in range(2)]

        def take(eng, s, n=1):
            eng.wait_ge(s, n).then_inc(s, -n)

        PAIRS = NB // 2
        loads = [
            (nvs[:], nv),
            (wfc1[:], w["W_fc1"]),
            (wfc2[:].rearrange("h (k f) -> h k f", k=2)[:, :, 0:S],
             w["W_fc2"][:, 0:2 * S].rearrange("h (k f) -> h k f", k=2)),
            (wfc2[:].rearrange("h (k f) -> h k f", k=2)[:, :, S:MID],
             w["W_fc2"][:, 2 * S:2 * MID].rearrange("h (k f) -> h k f", k=2)),
            (wl3s[:], w["Ws_l3"]), (wl3v[:], w["Wv_l3"]),
            (wl2[:, 0, :], w["Ws_l2_aT"]), (wl2[:, 1, :], w["Ws_l2_cT"]),
            (wl2[:, 2, :], w["Wv_l2_aT"]), (wl2[:, 3, :], w["Wv_l2_cT"]),
            (dst_i, dst_t), (attr[:], attr_t),
        ]
        wn_loads = []
        blocks = wn[:].rearrange("p (k t u) -> p k t u", k=5, t=2)
        for t, step in enumerate(("l1", "sc")):
            for h, kind in enumerate("ac"):
                ws, wv = w[f"Ws_{step}_{kind}"], w[f"Wv_{step}_{kind}"]
                for k in range(2):
                    wn_loads += [(blocks[64 * k + 32 * h:64 * k + 32 * h + 32, 0:2, t, :],
                                  ws[32 * k:32 * k + 32, :].rearrange("p (k u) -> p k u", k=2)),
                                 (blocks[64 * k + 32 * h:64 * k + 32 * h + 32, 2 + k, t, :], wv)]
                wn_loads += [(blocks[32 * h:32 * h + 32, 4, t, :], wv)]
        N_LOADS = 16 * len(loads)

        def load_range(eng, word, b):
            eng.reg_load(word, row[0:1, bass.ds(b * 2, 1)])

        def unpack(eng, word):
            word = eng.snap(word)
            mask = (1 << RB) - 1
            first = eng.snap(word & mask).with_bounds(min_val=0, max_val=U - 1)
            count = eng.snap((word >> RB) & mask).with_bounds(min_val=1, max_val=U)
            return first, count, eng.snap(word >> (2 * RB)).with_bounds(min_val=0, max_val=RING - 1)

        def all_pairs(eng):
            return eng.value_load(row[0:1, NB * 2 - 1:NB * 2], min_val=NB, max_val=NB * U)

        def windows(eng, begin, pair, stages, finish=lambda: None):
            word = eng.alloc_register("window_word")
            load_range(eng, word, 0)

            def step(b, q, lags):
                first, count, phase = unpack(eng, word)
                begin(b, q, lags)
                pair(0, q, first, 0, phase)
                load_range(eng, word, b + 1)
                twos = eng.snap((count - 1) >> 1).with_bounds(min_val=0, max_val=U // 2)
                with eng.If(twos > 0):
                    with eng.Fori(0, twos) as i:
                        pair(1, q, first, i * 2 + 1, phase)
                        pair(2, q, first, i * 2 + 2, phase)
                    eng.nop()
                with eng.If((count & 1) < 1):
                    pair(1, q, first, count - 1, phase)
                    eng.nop()
                stages(b, q, lags)

            for b in range(LAGS):
                step(b, b % 2, range(1, b + 1))
            with eng.Fori(LAGS // 2, PAIRS) as p:
                for q in range(2):
                    step(p * 2 + q, q, range(1, LAGS + 1))
            finish()
            for b in range(NB, NB + LAGS):
                begin(b, b % 2, range(b - NB + 1, LAGS + 1))
                stages(b, b % 2, range(b - NB + 1, LAGS + 1))

        block = ctx.enter_context(nc.Block())

        @block.sync
        def _(sp):
            sp.dma_start(dstu, dst_u).then_inc(dstu_loaded, 16)
            whole = x[0:(NB - 1) * P, :].rearrange("(w p) f -> p w f", p=P)
            for ch in range(NCH):
                a, z = ch * LN_CHUNK, min((ch + 1) * LN_CHUNK, NB - 1)
                sp.dma_start(base[:, a:z, :], whole[:, a:z, :]).then_inc(x_loaded[ch], 16)
            sp.dma_start(base[:, NB - 1, :], x[LAST:N, :]).then_inc(x_loaded[NCH - 1], 16)
            sp.wait_ge(zeroed, 1)
            for to, fr in wn_loads:
                sp.dma_start(to, fr).then_inc(wn_loaded, 16)
            for to, fr in loads:
                sp.dma_start(to, fr).then_inc(in_loaded, 16)
            sp.wait_ge(mm_done, 1)
            for k in range(2):
                sp.dma_start(tmm[k].rearrange("(p g) -> p g", g=UG), mm[:, k, :]).then_inc(mm_stored, 16)
            sp.wait_ge(mm_stored, 32)
            sp.dma_start(mmb, tmm.unsqueeze(0).to_broadcast([NB, 2, U])).then_inc(mm_loaded, 16)
            sp.wait_ge(rng_done, 1)
            sp.dma_start(rng, rngc[:]).then_inc(rng_stored, 16)
            sp.wait_ge(rng_stored, 16)
            sp.dma_start(row[:, 0:2 * NB], rng.rearrange("b k -> (b k)").unsqueeze(0)).then_inc(row_loaded, 16)
            for ch in range(NCH):
                a, z = ch * LN_CHUNK, min((ch + 1) * LN_CHUNK, NB - 1)
                sp.wait_ge(x1_ready, (z - a) + a)
                sp.dma_start(x1[0:(NB - 1) * P, :].rearrange("(w p) f -> p w f", p=P)[:, a:z, :],
                             xc[:, a:z, :]).then_inc(x1_stored, 16)
            sp.wait_ge(x1_ready, NB)
            sp.wait_ge(x1_stored, 16 * NCH)
            sp.dma_start(x1[LAST:N, :], xc[:, NB - 1, :]).then_inc(x1_stored, 16)

            sp.wait_ge(row_loaded, 16)
            sp.wait_ge(in_loaded, N_LOADS)

            def issue(way, slot, u):
                take(sp, idx_free)
                take(sp, len_free)
                sp.dma_start(idx[:, bass.ds(slot, 1), :].rearrange("p o j -> p (o j)"),
                             src_p[bass.ds(u, 1), :, :].rearrange("o p j -> p (o j)")).then_inc(loaded[way], 16)
                sp.dma_start(lenr[:, bass.ds(slot, 1), :].rearrange("p o e -> p (o e)"),
                             len_T[:, bass.ds(u * 2 * P, 2 * P)]).then_inc(loaded[way], 16)

            def pass_on(way):
                take(sp, loaded[way], 32)
                sp.sem_inc(idx_ready, 1)
                sp.sem_inc(len_ready, 1)

            def single(step, u):
                issue(2, sp.snap(step & (RING - 1)), u)
                pass_on(1)
                take(sp, loaded[2], 32)
                sp.sem_inc(loaded[1], 32)

            sp.sem_inc(loaded[1], 32)
            sp.sem_inc(idx_free, RING)
            sp.sem_inc(len_free, RING)
            word = sp.alloc_register("window_word")
            with sp.Fori(0, NB) as b:
                load_range(sp, word, b)
                first, count, phase = unpack(sp, word)
                twos = sp.snap(count >> 1).with_bounds(min_val=0, max_val=U // 2)
                with sp.If(twos > 0):
                    with sp.Fori(0, twos) as i:
                        for way in range(2):
                            step = i * 2 + way
                            issue(way, sp.snap((phase + step) & (RING - 1)),
                                  (first + step).with_bounds(min_val=0, max_val=U - 1))
                            pass_on(1 - way)
                    sp.nop()
                with sp.If((count & 1) > 0):
                    single(phase + count - 1, (first + count - 1).with_bounds(min_val=0, max_val=U - 1))
                    sp.nop()
            total = all_pairs(sp)
            with sp.Fori(0, sp.snap((((total + RING + AHEAD) >> RING_LOG) << RING_LOG) - total)) as i:
                single(total + i, i.with_bounds(min_val=0, max_val=RING + AHEAD))
            pass_on(1)

        @block.gpsimd
        def _(pool):
            nc.gpsimd.memset(wn[:], 0.0).then_inc(zeroed, 1)
            nc.gpsimd.iota(iota_i[:], [[1, P]], base=0, channel_multiplier=0).then_inc(iotas, 1)
            nc.gpsimd.iota(pos_i, [[1, U]], base=0, channel_multiplier=0).then_inc(iotas, 1)
            nc.gpsimd.memset(ident[:], 0.0).then_inc(iotas, 1)
            pool.wait_ge(iotas, 3)
            nc.gpsimd.affine_select(out=ident[:], in_=ident[:], compare_op=ALU.not_equal, fill=1.0, base=0,
                                    pattern=[[-1, P]], channel_multiplier=1).then_inc(consts, 1)
            nc.gpsimd.memset(tri[:], 1.0).then_inc(iotas, 1)
            pool.wait_ge(iotas, 4)
            nc.gpsimd.affine_select(out=tri[:], in_=tri[:], compare_op=ALU.is_gt, fill=0.0, base=0,
                                    pattern=[[1, NB]], channel_multiplier=-1).then_inc(consts, 1)
            nc.gpsimd.memset(zero[:], 0.0).then_inc(consts, 1)
            nc.gpsimd.memset(row[:, 2 * NB:], 0).then_inc(consts, 1)

            pool.wait_ge(row_loaded, 16)
            rounds = pool.snap((all_pairs(pool) + RING + AHEAD) >> RING_LOG)
            pool.wait_ge(x1_stored, 16 * (NCH + 1))

            def round_(g):
                for k in range(RING):
                    take(pool, idx_ready)
                    take(pool, g_free)
                    for j in range(2):
                        pool.indirect_dma_start(
                            out=G[:, k, j, :], out_offset=None, in_=x1,
                            in_offset=bass.IndirectOffsetOnAxis(ap=idx[:, k, j:j + 1], axis=0),
                        ).then_inc(gathered[k], 16)
                    if k >= LAG:
                        pool.wait_ge(gathered[k - LAG], g * 32 + 32).then_inc(g_ready, 1)
                        pool.sem_inc(idx_free, 1)
                    elif not isinstance(g, int):
                        pool.wait_ge(gathered[k - LAG + RING], g * 32).then_inc(g_ready, 1)
                        pool.sem_inc(idx_free, 1)

            take(pool, idx_ready)
            round_(0)
            with pool.Fori(1, rounds) as g:
                round_(g)
            for k in range(RING - LAG, RING):
                pool.wait_ge(gathered[k], rounds * 32).then_inc(g_ready, 1)
                pool.sem_inc(idx_free, 1)

        @block.scalar
        def _(act):
            for ch in range(NCH):
                a = ch * LN_CHUNK
                act.wait_ge(xc_ready, ch + 1)
                if ch >= 2:
                    act.wait_ge(var_done, ch - 1)
                nc.scalar.activation(sq[:, ch % 2].rearrange("p (w f) -> p w f", w=LN_CHUNK),
                                     xc[:, a:a + LN_CHUNK, :], ACT.Square).then_inc(sq_done, 1)
                nc.scalar.activation(xc[:, a:a + LN_CHUNK, :], xc[:, a:a + LN_CHUNK, :], ACT.Relu
                                     ).then_inc(relu_done, 1)
                if ch >= 1:
                    act.wait_ge(var_done, ch)
                    nc.scalar.activation(stat[:, (ch - 1) % 2, 3, :], stat[:, (ch - 1) % 2, 2, :],
                                         ACT.Sqrt).then_inc(std_done, 1)
            act.wait_ge(var_done, NCH)
            nc.scalar.activation(stat[:, (NCH - 1) % 2, 3, :], stat[:, (NCH - 1) % 2, 2, :],
                                 ACT.Sqrt).then_inc(std_done, 1)

            act.wait_ge(ln_done, 1)
            with act.Fori(0, PAIRS) as p:
                for q in range(2):
                    take(act, h_t)
                    if q == 1:
                        act.sem_inc(xs_free, 1)
                    nc.scalar.copy(hT[:, q, 0:2 * P], bank[q][:, 0:2 * P])
                    nc.scalar.copy(hT[0:2 * V, q, 2 * P:3 * P], bank[q][0:2 * V, 2 * P:3 * P]).then_inc(h_evac, 1)
                for q in range(2):
                    take(act, n_mm)
                    nc.scalar.copy(xc[:, bass.ds(p * 2 + q, 1), :].rearrange("p o (k u) -> p (o k) u", k=5),
                                   bank[2 + q][:, 0:2 * D].rearrange("p (k t u) -> p k t u", k=5, t=2)[:, :, 0, :]
                                   ).then_inc(n_x1, 1)

            act.wait_ge(fold_mm, 1)
            nc.scalar.activation(fold[0:64, 0:128], bank[6][0:64, 0:128], ACT.Copy)
            nc.scalar.activation(fold[64:96, 0:128], bank[6][64:96, 0:128], ACT.Copy, scale=1.0 / math.sqrt(3.0))
            nc.scalar.activation(fold[:, 128:192], bank[6][0:96, 128:192], ACT.Copy).then_inc(fold_done, 1)

            act.wait_ge(row_loaded, 16)
            act.wait_ge(consts, 4)

            def silu(j):
                take(act, pre_ready[j])
                if j == 1:
                    act.sem_inc(len_free, 1)
                nc.scalar.activation(hid[:, j, :], bank[7 * j][0:H, 0:P], ACT.Silu).then_inc(hid_ready[j], 1)

            def pair(r, q, first, i, phase):
                u2 = (first + i).with_bounds(min_val=0, max_val=U - 1) * 2
                take(act, wts_free[r])
                for j in range(2):
                    take(act, w_ready[j])
                    for c in range(4):
                        last = nc.scalar.activation(wts[:, r, j, c, :],
                                                    bank[1 + j][:, MID * (c > 0):MID * (c > 0) + MID], ACT.Copy,
                                                    scale=attr[:, bass.ds(u2 + j, 1), c])
                    if j == 1:
                        last.then_inc(wts_ready[r], 1)
                    silu(j)

            def stages(b, q, lags):
                if 4 in lags:
                    take(act, out_ready)
                    if isinstance(b, int) and b - 4 == NB - 1:
                        act.wait_ge(out_stored[1 - q], 16)
                    start = LAST if isinstance(b, int) and b - 4 == NB - 1 else (b - 4) * P
                    act.dma_start(out[bass.ds(start, P), :], outs[:, q, :]).then_inc(out_stored[q], 16)
                if 3 in lags:
                    take(act, o_mm)
                    act.sem_inc(o_ready, 1)
                if 2 in lags:
                    take(act, aggT_mm)
                    nc.scalar.copy(aggT[:], bank[4][0:MID, :]).then_inc(aggT_ready, 1)
                if 1 in lags:
                    take(act, sums_done)
                    sums = bank[3 + 3 * (1 - q)]
                    nc.scalar.copy(agg[:, :, 0:S], sums[:, 0:AB].rearrange("p (k f) -> p k f", k=4))
                    nc.scalar.copy(agg[:, 0, S:MID], sums[:, AB + CD:SUMS])
                    nc.scalar.copy(agg[:, 1:4, S:MID], sums[:, AB:AB + CD].rearrange("p (c u) -> p c u", c=3)
                                   ).then_inc(agg_copied, 1)

            def finish():
                for step in range(1, AHEAD):
                    for j in range(2):
                        take(act, w_ready[j])
                        silu(j)

            silu(0)
            silu(1)
            windows(act, lambda b, q, lags: None, pair, stages, finish)

        @block.vector
        def _(dve):
            def variance(ch):
                st = stat[:, ch % 2]
                dve.wait_ge(sq_done, ch + 1)
                nc.vector.reduce_sum(st[:, 0, :], sq[:, ch % 2].rearrange("p (w f) -> p w f", w=LN_CHUNK),
                                     axis=AX.X)
                dve.drain()
                nc.vector.tensor_scalar(st[:, 2, :], st[:, 0, :], 1.0 / D, 1e-5, ALU.mult,
                                        ALU.add).then_inc(var_done, 1)

            def inverse(ch):
                dve.wait_ge(std_done, ch + 1)
                nc.vector.reciprocal(rstd[:, ch * LN_CHUNK:(ch + 1) * LN_CHUNK], stat[:, ch % 2, 3, :])

            def norm(ch):
                a = ch * LN_CHUNK
                z = a + LN_CHUNK
                dve.wait_ge(x_loaded[ch], 16 * (1 + (ch == NCH - 1)))
                if ch >= 2:
                    inverse(ch - 2)
                    dve.drain()
                st = stat[:, ch % 2]
                nc.vector.reduce_sum(st[:, 0, :], base[:, a:z, :], axis=AX.X)
                dve.drain()
                nc.vector.tensor_scalar(st[:, 1, :], st[:, 0, :], 1.0 / D, None, ALU.mult)
                dve.drain()
                mean = st[:, 1, :]
                nc.vector.tensor_tensor(xc[:, a:z, 0:S], base[:, a:z, 0:S],
                                        mean.unsqueeze(2).to_broadcast([P, LN_CHUNK, S]), ALU.subtract)
                nc.vector.tensor_tensor(xc[:, a:z, S:D].rearrange("p w (c u) -> p w c u", c=3),
                                        base[:, a:z, S:D].rearrange("p w (u c) -> p w c u", c=3),
                                        mean.unsqueeze(2).unsqueeze(3).to_broadcast([P, LN_CHUNK, 3, V]),
                                        ALU.subtract).then_inc(xc_ready, 1)
                if ch >= 1:
                    variance(ch - 1)
            for ch in range(EARLY):
                norm(ch)

            dve.wait_ge(iotas, 2)
            nc.vector.tensor_copy(iota_f[:], iota_i[:])
            nc.vector.tensor_copy(pos, pos_i)
            dve.wait_ge(dstu_loaded, 16)
            nc.vector.tensor_reduce(mm[:, 0, :], dstu, AX.X, ALU.min)
            nc.vector.tensor_reduce(mm[:, 1, :], dstu, AX.X, ALU.max).then_inc(mm_done, 1)
            dve.drain()
            nc.vector.tensor_scalar(wst[:], iota_f[:, 0:NB + 1], float(P), float(LAST), ALU.mult, ALU.min)
            dve.wait_ge(consts, 1)
            nc.vector.tensor_tensor(iota_w[:, 0, :], iota_f[:], ident[:], ALU.mult)
            dve.drain()
            nc.vector.reduce_sum(part_f[:], iota_w[:, 0, :], axis=AX.X)
            dve.drain()
            nc.vector.tensor_scalar(wst_c[:, 0:1], part_f[0:NB, :], float(P), float(LAST), ALU.mult, ALU.min)
            dve.drain()
            nc.vector.tensor_scalar(wst_c[:, 1:2], wst_c[:, 0:1], float(P), None, ALU.add)
            dve.wait_ge(mm_loaded, 16)
            dve.drain()
            lo, hi = mmb[:, 0, :], mmb[:, 1, :]
            nc.vector.tensor_scalar(lo, lo, wst_c[:, 1:2], None, ALU.is_lt)
            dve.drain()
            nc.vector.scalar_tensor_tensor(out=lo, in0=hi, scalar=wst_c[:, 0:1], in1=lo, op0=ALU.is_ge, op1=ALU.mult)
            dve.drain()
            nc.vector.scalar_tensor_tensor(out=hi, in0=pos, scalar=1.0, in1=lo, op0=ALU.add, op1=ALU.mult)
            dve.drain()
            nc.vector.reduce_max(hl[:, 0:1], hi, axis=AX.X)
            dve.drain()
            nc.vector.tensor_scalar(pos, pos, -1.0, float(U), ALU.mult, ALU.add)
            dve.drain()
            nc.vector.tensor_tensor(hi, pos, lo, ALU.mult)
            dve.drain()
            nc.vector.reduce_max(hl[:, 1:2], hi, axis=AX.X)
            dve.drain()
            nc.vector.tensor_scalar(hl[:, 0:1], hl[:, 0:1], 1.0, None, ALU.max)
            nc.vector.tensor_scalar(hl[:, 1:2], hl[:, 1:2], -1.0, float(U), ALU.mult, ALU.add)
            dve.drain()
            nc.vector.tensor_scalar(hl[:, 2:3], hl[:, 0:1], 1.0, None, ALU.subtract)
            dve.drain()
            nc.vector.tensor_tensor(hl[:, 1:2], hl[:, 1:2], hl[:, 2:3], ALU.min)
            dve.drain()
            nc.vector.tensor_tensor(hl[:, 2:3], hl[:, 0:1], hl[:, 1:2], ALU.subtract).then_inc(cnt_done, 1)
            dve.wait_ge(cum_done, 1)
            nc.vector.tensor_copy(phase[:], bank[7][0:NB, 0:1])
            nc.vector.scalar_tensor_tensor(out=hl[:, 3:4], in0=hl[:, 2:3], scalar=float(1 << RB), in1=hl[:, 1:2],
                                           op0=ALU.mult, op1=ALU.add)
            dve.drain()
            nc.vector.tensor_scalar(phase[:], phase[:], RING - 1, 2 * RB, ALU.bitwise_and, ALU.logical_shift_left)
            nc.vector.tensor_tensor(rngc[:, 1:2], hl[:, 2:3], bank[7][0:NB, 0:1], ALU.add)
            dve.drain()
            nc.vector.tensor_tensor(rngc[:, 0:1], hl[:, 3:4], phase[:], ALU.add).then_inc(rng_done, 1)

            dve.wait_ge(in_loaded, N_LOADS)
            nc.vector.tensor_copy(dstf[:], dst_i)
            dve.drain()

            for ch in range(EARLY, NCH):
                norm(ch)
            variance(NCH - 1)
            inverse(NCH - 2)
            inverse(NCH - 1)
            dve.drain()
            for k in range(2):
                nc.vector.tensor_tensor(arcr[:, k, :], nvs[:, k, :], rstd[:], ALU.mult)
                nc.vector.scalar_tensor_tensor(out=uauc[:, k, :], in0=nvs[:, k, :], scalar=C_X / AVG,
                                               in1=nvs[:, 2, :], op0=ALU.mult, op1=ALU.mult)
            dve.wait_ge(relu_done, NCH)
            dve.wait_ge(wn_loaded, 16 * len(wn_loads))
            nc.vector.tensor_scalar(blocks[:, :, 1, :], blocks[:, :, 1, :], C_S, None, ALU.mult).then_inc(wn_scaled, 1)
            dve.drain().then_inc(ln_done, 1)

            def node_input(p):
                take(dve, xs_free)
                for k in range(2):
                    last = nc.vector.tensor_tensor(
                        xs.rearrange("p q (k t u) -> p q k t u", k=5, t=2)[:, :, :, k, :],
                        xc[:, bass.ds(p * 2, 2), :].rearrange("p q (k u) -> p q k u", k=5),
                        arcr[:, k, bass.ds(p * 2, 2)].unsqueeze(2).unsqueeze(3).to_broadcast([P, 2, 5, V]),
                        ALU.mult)
                last.then_inc(xs_ready, 1)

            def node_output(p):
                for q in range(2):
                    take(dve, n_x1)
                    dve.sem_inc(x1_ready, 1)
                    sc = bank[2 + q][:, 0:2 * D].rearrange("p (k t u) -> p k t u", k=5, t=2)[:, :, 1, :]
                    bw = base[:, bass.ds(p * 2 + q, 1), :].rearrange("p o f -> p (o f)")
                    bs = bw[:, 0:S].rearrange("p (k u) -> p k u", k=2)
                    nc.vector.tensor_tensor(bs, bs, sc[:, 0:2], ALU.add)
                    bv = bw[:, S:D].rearrange("p (u c) -> p c u", c=3)
                    nc.vector.tensor_tensor(bv, bv, sc[:, 2:5], ALU.add).then_inc(n_done[q], 1)

            dve.sem_inc(xs_free, 1)
            node_input(0)
            with dve.Fori(1, PAIRS) as p:
                node_input(p)
                node_output(p - 1)
            node_output(PAIRS - 1)

            dve.wait_ge(row_loaded, 16)
            dve.wait_ge(consts, 4)
            for r in range(BUFS):
                dve.sem_inc(prod_free[r], 1)
                dve.sem_inc(wts_free[r], 1)
            for q in range(2):
                dve.sem_inc(out_stored[q], 16)
            dve.sem_inc(g_free, RING)
            dve.sem_inc(o_free, 1)
            nc.vector.tensor_scalar(iota_w[:, 0, :], iota_f[:], wst[:, 0:1], None, ALU.add)
            dve.drain()

            def pair(r, q, first, i, phase):
                u2 = (first + i).with_bounds(min_val=0, max_val=U - 1) * 2
                slot = dve.snap((phase + i) & (RING - 1))
                g = G[:, bass.ds(slot, 1), :, :].rearrange("p o j f -> p (o j) f")
                gv = g[:, :, S:D].rearrange("p j (c u) -> p j c u", c=3)
                take(dve, prod_free[r])
                nc.vector.tensor_tensor(hot[:, r], iota_w[:, q, :].unsqueeze(1).to_broadcast([P, 2, P]),
                                        dstf[:, bass.ds(u2, 2)].unsqueeze(2).to_broadcast([P, 2, P]), ALU.is_equal)
                take(dve, g_ready)
                take(dve, wts_ready[r])
                nc.vector.tensor_tensor(dot[:, r].rearrange("p j (c u) -> p j c u", c=3), gv,
                                        wts[:, r, :, 1:4, S:MID], ALU.mult).then_inc(dot_done, 1)
                nc.vector.tensor_tensor(prod[:, r, :, 0:AB].rearrange("p j (k f) -> p j k f", k=4),
                                        wts[:, r, :, :, 0:S], g[:, :, 0:S].unsqueeze(2).to_broadcast([P, 2, 4, S]),
                                        ALU.mult)
                nc.vector.tensor_tensor(prod[:, r, :, AB:AB + CD].rearrange("p j (c u) -> p j c u", c=3), gv,
                                        wts[:, r, :, 0:1, S:MID].to_broadcast([P, 2, 3, V]), ALU.mult
                                        ).then_inc(wts_free[r], 1)
                take(dve, dot_done)
                nc.vector.tensor_reduce(prod[:, r, :, AB + CD:SUMS], dot[:, r].rearrange("p j (c u) -> p j u c", c=3),
                                        AX.X, ALU.add).then_inc(prod_ready[r], 1)

            def stages(b, q, lags):
                if not isinstance(b, int) or b + 1 < NB:
                    nc.vector.tensor_scalar(iota_w[:, 1 - q, :], iota_f[:], wst[:, bass.ds(b + 1, 1)], None, ALU.add)
                    dve.drain()
                if 3 in lags:
                    take(dve, out_stored[1 - q], 16)
                    take(dve, o_ready)
                    bw = base[:, bass.ds(b - 3, 1), :].rearrange("p o f -> p (o f)")
                    nc.vector.scalar_tensor_tensor(out=outs[:, 1 - q, :], in0=bank[5][:, 0:D],
                                                   scalar=uauc[:, 0, bass.ds(b - 3, 1)], in1=bw,
                                                   op0=ALU.mult, op1=ALU.add)
                    dve.drain()
                    nc.vector.scalar_tensor_tensor(out=outs[:, 1 - q, :], in0=bank[5][:, D:2 * D],
                                                   scalar=uauc[:, 1, bass.ds(b - 3, 1)], in1=outs[:, 1 - q, :],
                                                   op0=ALU.mult, op1=ALU.add).then_inc(out_ready, 1)
                    dve.drain().then_inc(o_free, 1)

            windows(dve, lambda b, q, lags: None, pair, stages)
            take(dve, out_stored[(NB - 1) % 2], 16)
            take(dve, out_stored[NB % 2], 16)

        @block.tensor
        def _(pe):
            pe.wait_ge(cnt_done, 1)
            pe.wait_ge(consts, 4)
            nc.tensor.matmul(bank[7][0:NB, 0:1], tri[:], hl[:, 2:3], start=True, stop=True).then_inc(cum_done, 1)
            pe.wait_ge(in_loaded, N_LOADS)
            for k in range(2):
                nc.tensor.matmul(bank[6][0:MID, S * k:S * (k + 1)], wl2[:, k, :], wl3s[:], start=True, stop=True)
            for k in range(2):
                last = nc.tensor.matmul(bank[6][0:MID, 128 + V * k:128 + V * (k + 1)], wl2[:, 2 + k, :], wl3v[:],
                                        start=True, stop=True)
            last.then_inc(fold_mm, 1)

            pe.wait_ge(ln_done, 1)
            pe.wait_ge(wn_scaled, 1)
            for q in range(2):
                pe.sem_inc(n_done[q], 1)
            with pe.Fori(0, PAIRS) as p:
                take(pe, xs_ready)
                for q in range(2):
                    for k in range(2):
                        nc.tensor.transpose(bank[q][:, P * k:P * (k + 1)], xs[:, q, P * k:P * (k + 1)], ident[:])
                    nc.tensor.transpose(bank[q][0:2 * V, 2 * P:3 * P], xs[:, q, 2 * P:2 * D], ident[:]
                                        ).then_inc(h_t, 1)
                for q in range(2):
                    take(pe, h_evac)
                    take(pe, n_done[q])
                    for k in range(2):
                        nc.tensor.matmul(bank[2 + q][:, P * k:P * (k + 1)], hT[:, q, P * k:P * (k + 1)],
                                         wn[:, P * k:P * (k + 1)], start=True, stop=True, skip_group_check=True)
                    nc.tensor.matmul(bank[2 + q][:, 2 * P:2 * D], hT[0:2 * V, q, 2 * P:3 * P],
                                     wn[0:2 * V, 2 * P:2 * D], start=True, stop=True,
                                     skip_group_check=True).then_inc(n_mm, 1)
            for q in range(2):
                take(pe, n_done[q])

            def first_map(step, j):
                if j == 0:
                    take(pe, len_ready)
                slot = pe.snap(step & (RING - 1))
                nc.tensor.matmul(bank[7 * j][0:H, 0:P], wfc1[:],
                                 lenr[:, bass.ds(slot, 1), P * j:P * (j + 1)].rearrange("p o e -> p (o e)"),
                                 start=True, stop=True).then_inc(pre_ready[j], 1)

            def maps(step, j):
                take(pe, hid_ready[j])
                nc.tensor.matmul(bank[1 + j][:, 0:2 * MID], hid[:, j, :], wfc2[:], start=True,
                                 stop=True).then_inc(w_ready[j], 1)
                first_map(step + 1, j)

            def begin(b, q, lags):
                if 3 in lags:
                    take(pe, aggT_ready)
                    take(pe, o_free)
                    o = bank[5][:, 0:2 * D].rearrange("p (k f) -> p k f", k=2)
                    nc.tensor.matmul(o[:, :, 0:S], aggT[:, 0:P], fold[:, 0:2 * S], start=True, stop=True,
                                     skip_group_check=True)
                    ov = o[:, :, S:D].rearrange("p k (u c) -> p k u c", c=3)
                    for c in range(3):
                        last = nc.tensor.matmul(ov[:, :, :, c], aggT[:, P * (c + 1):P * (c + 2)],
                                                fold[:, 2 * S:2 * S + 2 * V], start=True, stop=True,
                                                skip_group_check=True)
                    last.then_inc(o_mm, 1)
                if 1 in lags:
                    nc.tensor.matmul(bank[3 + 3 * q][:, 0:1], zero[:, 0:P], zero[:, 0:1], start=True, stop=True,
                                     skip_group_check=True).then_inc(sums_done, 1)

            def pair(r, q, first, i, phase):
                for j in range(2):
                    maps(phase + i + AHEAD, j)
                    if j == 0:
                        take(pe, prod_ready[r])
                        pe.sem_inc(g_free, 1)
                    last = nc.tensor.matmul(bank[3 + 3 * q][:, 0:SUMS], hot[:, r, j, :], prod[:, r, j, :],
                                            start=(r == 0 and j == 0), stop=(j == 1), skip_group_check=True)
                last.then_inc(prod_free[r], 1)

            def stages(b, q, lags):
                if 1 in lags:
                    take(pe, agg_copied)
                    for k in range(4):
                        last = nc.tensor.transpose(bank[4][0:MID, P * k:P * (k + 1)], agg[:, k, :], ident[:])
                    last.then_inc(aggT_mm, 1)

            pe.wait_ge(fold_done, 1)
            take(pe, len_ready)
            first_map(0, 0)
            first_map(0, 1)
            for step in range(AHEAD):
                for j in range(2):
                    maps(step, j)
            windows(pe, begin, pair, stages)
            pe.sem_inc(g_free, AHEAD)


def kernel(**inputs):
    import numpy as np
    import concourse.bacc as bacc
    from concourse.bass_utils import run_bass_kernel_spmd as run

    a = {k: np.asarray(v) for k, v in inputs.items()}

    def edges(v):
        return np.pad(v, [(0, EP - E)] + [(0, 0)] * (v.ndim - 1), mode="edge")

    def lanes(v):
        v = v.reshape(2 * U, P, *v.shape[1:])
        return np.swapaxes(v, 0, 1)

    def windows(v):
        return np.concatenate([v[:(NB - 1) * P, 0].reshape(NB - 1, P).T, v[LAST:]], axis=1)

    arrays = {
        "x": a["x"],
        "dst_u": edges(a["dst"]).reshape(UP, UG, 2 * P),
        "dst_t": lanes(edges(a["dst"])),
        "src_p": np.swapaxes(edges(a["src"]).reshape(U, 2, P), 1, 2),
        "attr_t": lanes(np.pad(a["edge_attr_4"], [(0, EP - E), (0, 0)])),
        "len_T": edges(a["edge_attr_10"]).T,
        "nv": np.stack([windows(a[k]) for k in ("node_vec1", "node_vec1_n2", "node_vec1_n3")], axis=1),
    }
    weights = {}
    for k, v in a.items():
        if k.startswith("L0_gnn_"):
            k = k[len("L0_gnn_"):]
            if "_l2_" in k:
                k, v = k + "T", v.T
            weights[k] = v
    nc = bacc.Bacc("TRN2", target_bir_lowering=False, num_devices=1)
    feed = {}

    def dram(name, v):
        v = np.ascontiguousarray(v)
        feed["in_" + name] = v
        return nc.dram_tensor("in_" + name, v.shape, mybir.dt.from_np(v.dtype), kind="ExternalInput").ap()

    args = {k: dram(k, v) for k, v in arrays.items()}
    w = {k: dram(k, v) for k, v in weights.items()}
    out = nc.dram_tensor("out", (N, D), fp32, kind="ExternalOutput").ap()
    gnn_kernel(nc, **args, w=w, out=out)
    return run(nc, [feed], core_ids=[0]).results[0]["out"]
```
